# Optimizing a Trainium2 kernel written in Bass

```python
import numpy as np
import jax
import jax.numpy as jnp

def _softmax(x, axis=-1):
    return jax.nn.softmax(x, axis=axis)

def _gelu(x):
    return jax.nn.gelu(x, approximate=True)

def _silu(x):
    return jax.nn.silu(x)

def _sigmoid(x):
    return jax.nn.sigmoid(x)

def _layernorm(x, axis=-1, eps=1e-05):
    m = jnp.mean(x, axis=axis, keepdims=True)
    v = jnp.var(x, axis=axis, keepdims=True)
    return (x - m) / jnp.sqrt(v + eps)

def _scatter_add(tgt, idx, src, axis=0):
    return tgt.at[idx].add(src)

def _segment_sum(src, seg, n):
    return jax.ops.segment_sum(src, seg, n)
kernel_name = 'mk_prb_d1_jaxref_r8_6170c3'

def setup_inputs(seed: int=0):
    np.random.seed(seed)
    _w = jnp.asarray

    def _L0_attn_setup():
        import jax, jax.numpy as jnp
        import numpy as np
        N_HEAD = 8
        HEAD = 64
        RATIO = 2
        DEG = 2
        N_EMBD = 128
        QKV = (RATIO + 2) * N_HEAD * HEAD

        def _rope(t):
            B, T, h, d = t.shape
            div = 2.0 * np.pi / float(T) ** (np.arange(0, d, 2, dtype=np.float32) / d)
            ang = jnp.arange(T, dtype=jnp.float32)[:, None] * jnp.asarray(div)[None, :]
            sin = jnp.repeat(jnp.sin(ang), 2, axis=-1)[None, :, None, :]
            cos = jnp.repeat(jnp.cos(ang), 2, axis=-1)[None, :, None, :]
            x1 = t[..., ::2]
            x2 = t[..., 1::2]
            rot = jnp.stack((-x2, x1), axis=-1).reshape(t.shape)
            return t * cos + rot * sin
        key = jax.random.key(seed)
        k1, k2, k3 = jax.random.split(key, 3)
        B, T = (1, 256)
        x = jax.random.normal(k1, (B, T, N_EMBD), dtype=jnp.float32)
        w_attn = jax.random.normal(k2, (N_EMBD, QKV + N_HEAD), dtype=jnp.float32) * N_EMBD ** (-0.5)
        w_proj = jax.random.normal(k3, (RATIO * N_HEAD * HEAD, N_EMBD), dtype=jnp.float32) * (RATIO * N_HEAD * HEAD) ** (-0.5)
        ln_w = jnp.ones((HEAD,), dtype=jnp.float32)
        return {'x': x, 'w_attn': w_attn, 'w_proj': w_proj, 'ln_w': ln_w}
    _L0_attn_in = _L0_attn_setup()

    def _L0_ffn_setup():
        import jax, jax.numpy as jnp
        import numpy as np
        import math
        D_MODEL = 128
        D_FF = 512
        NUM_EXPERTS = 8
        NUM_SHARED = 1
        E_ROUTED = NUM_EXPERTS - NUM_SHARED
        TOP_K = 2
        CAP_FACTOR = 1.25
        B, S = (4, 256)
        T = B * S
        CAPACITY = math.ceil(CAP_FACTOR * T * TOP_K / E_ROUTED)
        SHARED_SCALE = 1.0

        def _layernorm(x, g, b, eps=1e-05):
            mu = jnp.mean(x, axis=-1, keepdims=True)
            var = jnp.mean((x - mu) ** 2, axis=-1, keepdims=True)
            return (x - mu) * jax.lax.rsqrt(var + eps) * g + b
        key = jax.random.key(seed)
        ks = jax.random.split(key, 10)
        s = 0.02
        return {'x': jax.random.normal(ks[0], (B, S, D_MODEL), dtype=jnp.float32), 'ln_g': jnp.ones((D_MODEL,), jnp.float32), 'ln_b': jnp.zeros((D_MODEL,), jnp.float32), 'Wr': jax.random.normal(ks[1], (D_MODEL, E_ROUTED), jnp.float32) * s, 'W1': jax.random.normal(ks[2], (E_ROUTED, D_MODEL, D_FF), jnp.float32) * s, 'W3': jax.random.normal(ks[3], (E_ROUTED, D_MODEL, D_FF), jnp.float32) * s, 'W2': jax.random.normal(ks[4], (E_ROUTED, D_FF, D_MODEL), jnp.float32) * s, 'W1s': jax.random.normal(ks[5], (D_MODEL, D_FF), jnp.float32) * s, 'W3s': jax.random.normal(ks[6], (D_MODEL, D_FF), jnp.float32) * s, 'W2s': jax.random.normal(ks[7], (D_FF, D_MODEL), jnp.float32) * s}
    _L0_ffn_in = _L0_ffn_setup()
    _d = {'L0_attn_x': _L0_attn_in['x'], 'L0_attn_w_attn': _L0_attn_in['w_attn'], 'L0_attn_w_proj': _L0_attn_in['w_proj'], 'L0_attn_ln_w': _L0_attn_in['ln_w'], 'L0_ffn_ln_g': _L0_ffn_in['ln_g'], 'L0_ffn_ln_b': _L0_ffn_in['ln_b'], 'L0_ffn_Wr': _L0_ffn_in['Wr'], 'L0_ffn_W1': _L0_ffn_in['W1'], 'L0_ffn_W3': _L0_ffn_in['W3'], 'L0_ffn_W2': _L0_ffn_in['W2'], 'L0_ffn_W1s': _L0_ffn_in['W1s'], 'L0_ffn_W3s': _L0_ffn_in['W3s'], 'L0_ffn_W2s': _L0_ffn_in['W2s']}
    _x0 = _d['L0_attn_x']
    _d['L0_attn_x'] = jax.random.normal(jax.random.fold_in(jax.random.key(seed), 1), (4, 1024, 128), dtype=_x0.dtype)
    del _x0
    return _d

def reference(L0_attn_x, L0_attn_w_attn, L0_attn_w_proj, L0_attn_ln_w, L0_ffn_ln_g, L0_ffn_ln_b, L0_ffn_Wr, L0_ffn_W1, L0_ffn_W3, L0_ffn_W2, L0_ffn_W1s, L0_ffn_W3s, L0_ffn_W2s):

    def _L0_attn_ref(x, w_attn, w_proj, ln_w):
        import jax, jax.numpy as jnp
        import numpy as np
        N_HEAD = 8
        HEAD = 64
        RATIO = 2
        DEG = 2
        N_EMBD = 128
        QKV = (RATIO + 2) * N_HEAD * HEAD

        def _rope(t):
            B, T, h, d = t.shape
            div = 2.0 * np.pi / float(T) ** (np.arange(0, d, 2, dtype=np.float32) / d)
            ang = jnp.arange(T, dtype=jnp.float32)[:, None] * jnp.asarray(div)[None, :]
            sin = jnp.repeat(jnp.sin(ang), 2, axis=-1)[None, :, None, :]
            cos = jnp.repeat(jnp.cos(ang), 2, axis=-1)[None, :, None, :]
            x1 = t[..., ::2]
            x2 = t[..., 1::2]
            rot = jnp.stack((-x2, x1), axis=-1).reshape(t.shape)
            return t * cos + rot * sin
        B, T, C = x.shape
        h, d, r = (N_HEAD, HEAD, RATIO)
        hq = r * h
        qkvg = x @ w_attn
        q = qkvg[..., :hq * d].reshape(B, T, hq, d)
        k = qkvg[..., hq * d:(hq + h) * d].reshape(B, T, h, d)
        v = qkvg[..., (hq + h) * d:QKV].reshape(B, T, h, d)
        log_g = jax.nn.log_sigmoid(6.906768 + qkvg[..., QKV:])
        q = _rope(q)
        k = _rope(k)
        k = jnp.repeat(k, r, axis=2)
        v = jnp.repeat(v, r, axis=2)
        log_G = jnp.repeat(jnp.cumsum(log_g, axis=1), r, axis=2).transpose(0, 2, 1)
        scale = 1.0 / d ** 0.5
        s = jnp.einsum('bthd,bshd->bhts', q, k) * scale
        logits = DEG * jnp.log(jnp.abs(s) + 1e-30) + log_G[:, :, :, None] - log_G[:, :, None, :]
        mask = jnp.tril(jnp.ones((T, T), dtype=bool))
        logits = jnp.where(mask, logits, -jnp.inf)
        m = jax.lax.stop_gradient(jnp.max(logits, axis=-1, keepdims=True))
        a = jnp.exp(logits - m)
        if DEG % 2 == 1:
            a = a * jnp.sign(s)
        a = jnp.where(mask, a, 0.0)
        num = jnp.einsum('bhts,bshd->bthd', a, v)
        den = jnp.sum(a, axis=-1).transpose(0, 2, 1)
        y = num / (den[..., None] + 1e-06)
        mu = jnp.mean(y, axis=-1, keepdims=True)
        var = jnp.mean((y - mu) ** 2, axis=-1, keepdims=True)
        y = (y - mu) / jnp.sqrt(var + 1e-09) * ln_w
        return y.reshape(B, T, hq * d) @ w_proj

    def _L0_ffn_ref(x, ln_g, ln_b, Wr, W1, W3, W2, W1s, W3s, W2s):
        import jax, jax.numpy as jnp
        import numpy as np
        import math
        D_MODEL = 128
        D_FF = 512
        NUM_EXPERTS = 8
        NUM_SHARED = 1
        E_ROUTED = NUM_EXPERTS - NUM_SHARED
        TOP_K = 2
        CAP_FACTOR = 1.25
        B, S = (4, 256)
        T = B * S
        CAPACITY = math.ceil(CAP_FACTOR * T * TOP_K / E_ROUTED)
        SHARED_SCALE = 1.0

        def _layernorm(x, g, b, eps=1e-05):
            mu = jnp.mean(x, axis=-1, keepdims=True)
            var = jnp.mean((x - mu) ** 2, axis=-1, keepdims=True)
            return (x - mu) * jax.lax.rsqrt(var + eps) * g + b
        Bx, Sx, D = x.shape
        Tn = Bx * Sx
        h = _layernorm(x, ln_g, ln_b).reshape(Tn, D)
        logits = h @ Wr
        top_vals, top_idx = jax.lax.top_k(logits, TOP_K)
        gates = jax.nn.softmax(top_vals, axis=-1)
        idx = top_idx.T.reshape(-1)
        gat = gates.T.reshape(-1)
        tok = jnp.tile(jnp.arange(Tn), TOP_K)
        onehot = jax.nn.one_hot(idx, E_ROUTED, dtype=jnp.int32)
        pos = jnp.sum(jnp.cumsum(onehot, axis=0) * onehot, axis=-1) - 1
        keep = pos < CAPACITY
        pos_c = jnp.where(keep, pos, CAPACITY)
        xe = jnp.zeros((E_ROUTED, CAPACITY, D), h.dtype).at[idx, pos_c].set(h[tok], mode='drop')
        a = jnp.einsum('ecd,edf->ecf', xe, W1)
        b = jnp.einsum('ecd,edf->ecf', xe, W3)
        ye = jnp.einsum('ecf,efd->ecd', jax.nn.silu(a) * b, W2)
        out_slots = ye[jnp.clip(idx, 0, E_ROUTED - 1), jnp.clip(pos_c, 0, CAPACITY - 1)]
        out_slots = out_slots * (gat * keep.astype(gat.dtype))[:, None]
        routed = jnp.zeros((Tn, D), h.dtype).at[tok].add(out_slots)
        shared = jax.nn.silu(h @ W1s) * (h @ W3s) @ W2s
        out = routed + SHARED_SCALE * shared
        return out.reshape(Bx, Sx, D)
    x = L0_attn_x
    xn = _layernorm(x, axis=-1)
    x = x + _L0_attn_ref(xn, L0_attn_w_attn, L0_attn_w_proj, L0_attn_ln_w) + _L0_ffn_ref(xn, L0_ffn_ln_g, L0_ffn_ln_b, L0_ffn_Wr, L0_ffn_W1, L0_ffn_W3, L0_ffn_W2, L0_ffn_W1s, L0_ffn_W3s, L0_ffn_W2s)
    return x

_drawn_inputs = setup_inputs


def setup_inputs(seed=0):
    import zlib

    import numpy as np

    out = dict(_drawn_inputs(seed))
    spreads = {'L0_attn_ln_w': (1.0, 0.6), 'L0_ffn_ln_g': (1.0, 0.6), 'L0_ffn_ln_b': (0.0, 0.8)}
    factors = {'L0_ffn_Wr': 8.0,
     'L0_ffn_W1': 8.0,
     'L0_ffn_W3': 8.0,
     'L0_ffn_W2': 8.0,
     'L0_ffn_W1s': 6.336,
     'L0_ffn_W3s': 6.275,
     'L0_ffn_W2s': 6.277}
    for name, (base, spread) in spreads.items():
        noise = np.random.default_rng([zlib.crc32(name.encode()), seed]).standard_normal(out[name].shape)
        drawn = base * np.exp(spread * noise) if base else spread * noise
        out[name] = jnp.asarray(drawn.astype(out[name].dtype))
    for name, factor in factors.items():
        out[name] = (out[name] * factor).astype(out[name].dtype)
    return out
```

```python
import math
from contextlib import ExitStack

import numpy as np

import concourse.bass as bass
from concourse import mybir
from concourse.alu_op_type import AluOpType as ALU

B, T, C = 4, 1024, 128
NB = 8
NBLK = B * NB
KVH = 8
HD = 64
NE = 7
CAP = 366
SLOT = 384
FF = 512
LAG = 2
GUARD = 1e-15
CLAMP = 60.0

C_ID, C_UT, C_US, C_ONE, C_H, C_IM8, C_I384, C_COS, C_SIN = 0, 128, 256, 384, 512, 576, 584, 592, 1104
NCONST = 1616


def block_program(nc, x, w_qkv, w_gate, wvT, w_proj, ln_w2, ln_g, ln_b, wr, w1, w3, w2, w1s, w3s, w2s, const,
                  out):
    f32, f32r, u32 = mybir.dt.float32, mybir.dt.float32r, mybir.dt.uint32
    ACT = mybir.ActivationFunctionType
    AX = mybir.AxisListType.X
    v, s, te, g = nc.vector, nc.scalar, nc.tensor, nc.gpsimd

    xe_d = nc.dram_tensor("xe_d", (NE * SLOT, C), f32, kind="Internal").ap()
    ye_d = nc.dram_tensor("ye_d", (NE * SLOT, C), f32, kind="Internal").ap()
    H_d = nc.dram_tensor("H_d", (B * KVH * NB, 128), f32, kind="Internal").ap()

    ctx = ExitStack()
    with ctx:
        def sb(name, cols, dt=f32):
            return ctx.enter_context(nc.sbuf_tensor(name, [128, cols], dt))

        def sem(name):
            return ctx.enter_context(nc.semaphore(name))

        queues = {e: [] for e in ("pe", "act", "dve", "pool", "sp")}
        esem = {e: sem("s_" + e) for e in ("pe", "act", "dve", "pool")}
        count = {}

        def put(engine, f, waits, a, k, sm, by):
            waits = [w for w in waits if w is not None]
            queues[engine].append((f, waits, a, k, sm, by))
            if sm is None:
                return None
            count[sm.name] = count.get(sm.name, 0) + by
            return sm, count[sm.name]

        def PE(f, waits, *a, sig=False, **k):
            return put("pe", f, waits, a, k, esem["pe"] if sig else None, 1)

        def AC(f, waits, *a, **k):
            return put("act", f, waits, a, k, esem["act"], 1)

        def DV(f, waits, *a, **k):
            return put("dve", f, waits, a, k, esem["dve"], 1)

        def PO(f, waits, *a, **k):
            return put("pool", f, waits, a, k, esem["pool"], 1)

        def SPD(sm, waits, dst, src):
            return put("sp", nc.sync.dma_start, waits, (dst, src), {}, sm, 16)

        def POD(sm, f, waits, *a, **k):
            return put("pool", f, waits, a, k, sm, 16)

        def bc(ap, axis, n):
            shape = list(ap.shape)
            shape.insert(axis, n)
            return ap.unsqueeze(axis).broadcast_to(shape)

        K_ = sb("consts", NCONST)
        ident, utri, ustr, ones = (K_[:, o:o + 128] for o in (C_ID, C_UT, C_US, C_ONE))
        acc = sb("acc", NBLK * C)
        XTh, XTl = sb("XTh", NBLK * 128, f32r), sb("XTl", NBLK * 128, f32r)
        Wh, Wl = sb("Wh", 2048, f32r), sb("Wl", 2048, f32r)
        Wgh, Wgl = sb("Wgh", 8, f32r), sb("Wgl", 8, f32r)
        Wp = sb("Wp", 1024)
        GB = sb("GB", 256)
        WR = sb("WR", 16)
        negG = sb("negG", 256)
        ES, EB = sb("ES", 384), sb("EB", 384)
        gk = sb("gk", 64)
        idx_s, idx_g = sb("idx_s", 64, u32), sb("idx_g", 64, u32)
        SM = sb("SM", 1024)
        YG = sb("YG", 8 * 128)
        Kh = [sb(f"Kh{i}", 1024, f32r) for i in range(2)]
        Kl = [sb(f"Kl{i}", 1024, f32r) for i in range(2)]
        Qt = [sb(f"Qt{i}", 512, f32r) for i in range(3)]
        NU = 24832
        U = sb("U", NU)

        def carve():
            at = [0]

            def take(n):
                a = at[0]
                at[0] += n
                assert at[0] <= NU, at
                return U[:, a:a + n]
            return take

        take = carve()
        h_ = take(4096)
        hT = take(4096)
        XC = [take(1024) for _ in range(2)]
        SQ = take(1024)
        W32 = take(2048)
        wpr = take(2048)
        HL = take(64)
        wv_ = take(512)
        W1S, W3S, W2S = take(512), take(512), take(512)
        EW = [[take(512) for _ in range(3)] for _ in range(2)]
        XE = [take(384) for _ in range(2)]
        RW_ = take(2048)
        take = carve()
        take(8192)
        GT = [take(2048) for _ in range(2)]
        SIL = [take(512) for _ in range(2)]
        XET = [take(384) for _ in range(2)]
        YE = [take(384) for _ in range(2)]
        take = carve()
        QK = [take(3072) for _ in range(2)]
        ROT = [take(384) for _ in range(2)]
        Vt = [take(1024) for _ in range(2)]
        A = [take(512) for _ in range(6)]
        RUN = [take(512) for _ in range(2)]
        D = [take(1536) for _ in range(2)]
        HR = [take(1024) for _ in range(2)]
        NT = [take(256) for _ in range(2)]
        Y = [take(1024) for _ in range(2)]
        YN = take(1024)
        Y2 = take(1024)
        YT = [take(1024) for _ in range(2)]

        P = [ctx.enter_context(nc.psum_tensor(f"P{i}", [128, 512], f32)) for i in range(8)]

        s_c, s_w, s_hd, s_z, s_sc, s_ye, s_out = (sem(n) for n in ("s_c", "s_w", "s_hd", "s_z", "s_sc", "s_ye",
                                                                    "s_out"))
        s_wp, s_ws = sem("s_wp"), sem("s_ws")
        s_x = [sem(f"s_x{i}") for i in range(4)]
        s_ew = [sem(f"s_ew{i}") for i in range(2)]
        s_xe = [sem(f"s_xe{i}") for i in range(2)]
        s_hr = [sem(f"s_hr{i}") for i in range(2)]
        s_k = [[sem(f"s_k{i}{n}") for n in range(2)] for i in range(2)]
        s_yg = [sem(f"s_yg{i}") for i in range(8)]

        t_const = SPD(s_c, [], K_[:, :], const)
        x_v = x.rearrange("b (k p) c -> b p k c", p=128)
        out_v = out.rearrange("b (k p) c -> b p k c", p=128)
        acc_v = acc[:, :].rearrange("p (b k c) -> p b k c", b=B, k=NB)
        t_x = [SPD(s_x[b], [], acc_v[:, b], x_v[b]) for b in range(B)]
        SPD(s_w, [], W32.rearrange("p (u n) -> p u n", u=4)[:, :, 0:384], w_qkv)
        SPD(s_w, [], WR[:, 0:7], wr)
        SPD(s_w, [], WR[:, 8:16], w_gate)
        SPD(s_w, [], wv_.rearrange("p (u n) -> p u n", u=4), wvT)
        SPD(s_w, [], GB[:, 0:128], ln_g.partition_broadcast(128))
        t_w = SPD(s_w, [], GB[:, 128:256], ln_b.partition_broadcast(128))
        SPD(s_ws, [], W1S, w1s)
        SPD(s_ws, [], W3S, w3s)
        t_ws = SPD(s_ws, [], W2S.rearrange("p (c n) -> p c n", c=4), w2s.rearrange("(c p) n -> p c n", p=128))
        SPD(s_wp, [], wpr.rearrange("p (h n) -> p h n", h=16)[0:64], w_proj.rearrange("(h d) n -> d h n", d=64))
        t_wp = SPD(s_wp, [], HL[0:64, 0:1], ln_w2)

        def rsqrt(val, t_val, tmp, res):
            t = AC(s.activation, [t_val], tmp, val, ACT.Ln)
            t = AC(s.activation, [t], tmp, tmp, ACT.Exp, scale=-0.5)
            t1 = DV(v.tensor_tensor, [t, t_val], res, tmp, tmp, ALU.mult)
            t1 = DV(v.tensor_tensor, [t1], res, res, val, ALU.mult)
            t1 = DV(v.tensor_scalar, [t1], res, res, -0.5, 1.5, ALU.mult, ALU.add)
            return DV(v.tensor_tensor, [t1], res, res, tmp, ALU.mult)

        t_m = DV(v.memset, [], SQ, 0.0)
        xe_z = xe_d.rearrange("(a p) c -> p a c", p=128)
        zt = None
        for i in range(3):
            zt = SPD(s_z, [t_m], xe_z[:, 7 * i:7 * i + 7], SQ[:, 0:896].rearrange("p (a c) -> p a c", c=128))

        h_v = h_.rearrange("p (k c) -> p k c", c=128)
        t_h, t_xt, t_ht = [], [], []
        last_xt = [None] * 4
        sq_free, xc_free = [zt], [None, None]
        for b in range(B):
            x3 = acc_v[:, b]
            xc = XC[b % 2]
            xc3 = xc.rearrange("p (k c) -> p k c", c=128)
            sq3 = SQ.rearrange("p (k c) -> p k c", c=128)
            sm = SM[:, 64 * b:64 * b + 64]
            mean, var, tm, rs = (sm[:, 8 * i:8 * i + 8] for i in range(4))
            t = DV(v.tensor_reduce, [t_x[b]], mean, x3, AX, ALU.add)
            t = DV(v.tensor_scalar, [t], mean, mean, 1.0 / C, None, ALU.mult)
            t = DV(v.tensor_tensor, [t, xc_free[b % 2]], xc3, x3, bc(mean, 2, C), ALU.subtract)
            t2 = AC(s.activation, [t] + sq_free, SQ, xc, ACT.Square)
            t2 = DV(v.tensor_reduce, [t2], var, sq3, AX, ALU.add)
            t2 = DV(v.tensor_scalar, [t2], var, var, 1.0 / C, 1e-5, ALU.mult, ALU.add)
            t2 = rsqrt(var, t2, tm, rs)
            t_xn = DV(v.tensor_tensor, [t2], xc3, xc3, bc(rs, 2, C), ALU.mult)
            for i in range(2):
                bank = P[i]
                for q in range(4):
                    t = PE(te.transpose, [t_xn, t_const, last_xt[i]], bank[:, 128 * q:128 * q + 128],
                           xc[:, 512 * i + 128 * q:512 * i + 128 * q + 128], ident, sig=q == 3)
                o = 1024 * b + 512 * i
                ta = AC(s.activation, [t], XTh[:, o:o + 512], bank[:, :], ACT.Copy)
                last_xt[i] = DV(v.tensor_tensor, [ta], XTl[:, o:o + 512], bank[:, :],
                                XTh[:, o:o + 512].bitcast(f32), ALU.subtract)
                t_xt.append(last_xt[i])
            hb3 = h_v[:, NB * b:NB * b + NB]
            mean, var, tm, rs = (sm[:, 32 + 8 * i:40 + 8 * i] for i in range(4))
            t = DV(v.tensor_reduce, [t_xn], mean, xc3, AX, ALU.add)
            t = DV(v.tensor_scalar, [t], mean, mean, 1.0 / C, None, ALU.mult)
            t_hc = DV(v.tensor_tensor, [t], hb3, xc3, bc(mean, 2, C), ALU.subtract)
            xc_free[b % 2] = t_hc
            t2 = AC(s.activation, [t_hc], SQ, h_[:, 1024 * b:1024 * b + 1024], ACT.Square)
            t2 = DV(v.tensor_reduce, [t2], var, sq3, AX, ALU.add)
            sq_free = [t2]
            t2 = DV(v.tensor_scalar, [t2], var, var, 1.0 / C, 1e-5, ALU.mult, ALU.add)
            t2 = rsqrt(var, t2, tm, rs)
            t = DV(v.tensor_tensor, [t2], hb3, hb3, bc(rs, 2, C), ALU.mult)
            t = DV(v.tensor_tensor, [t, t_w], hb3, hb3, bc(GB[:, 0:128], 1, NB), ALU.mult)
            t = DV(v.tensor_tensor, [t], hb3, hb3, bc(GB[:, 128:256], 1, NB), ALU.add)
            t_h.append(t)
            for i in range(2):
                bank = P[2 + i]
                for q in range(4):
                    o = 1024 * b + 512 * i + 128 * q
                    t = PE(te.transpose, [t_h[b], last_xt[2 + i]], bank[:, 128 * q:128 * q + 128],
                           h_[:, o:o + 128], ident, sig=q == 3)
                o = 1024 * b + 512 * i
                last_xt[2 + i] = AC(s.activation, [t], hT[:, o:o + 512], bank[:, :], ACT.Copy)
                t_ht.append(last_xt[2 + i])

        for k in range(NBLK):
            t_lg = PE(te.matmul, [t_ht[k // 4], t_w], P[4][:, 8 * k:8 * k + 7], hT[:, 128 * k:128 * k + 128],
                      WR[:, 0:7], start=True, stop=True, sig=k == NBLK - 1)

        t_g0 = AC(s.activation, [t_w], Wgh[:, :], WR[:, 8:16], ACT.Copy)
        t_wg = DV(v.tensor_tensor, [t_g0], Wgl[:, :], WR[:, 8:16], Wgh[:, :].bitcast(f32), ALU.subtract)
        W4 = W32.rearrange("p (u n) -> p u n", u=4)
        for hh in range(2):
            for u in range(4):
                t = PE(te.matmul, [t_w, t_const], P[5 + 2 * hh][:, 64 * u:64 * u + 64],
                       wv_[64 * hh:64 * hh + 64, 128 * u:128 * u + 128], K_[64 * hh:64 * hh + 64, C_H:C_H + 64],
                       start=True, stop=True, sig=u == 3)
            t = AC(s.activation, [t], W4[:, :, 384 + 64 * hh:448 + 64 * hh],
                   P[5 + 2 * hh][:, 0:256].rearrange("p (u n) -> p u n", u=4), ACT.Copy)
        t_p5 = t
        t = AC(s.activation, [t], Wh[:, :], W32, ACT.Copy)
        t_wq = DV(v.tensor_tensor, [t], Wl[:, :], W32, Wh[:, :].bitcast(f32), ALU.subtract)
        gate_terms = ((XTh, Wgh), (XTh, Wgl), (XTl, Wgh))
        for k in range(NBLK):
            for i, (xt, wg) in enumerate(gate_terms):
                t_z = PE(te.matmul, [t_xt[k // 4], t_wg], P[6][:, 8 * k:8 * k + 8], xt[:, 128 * k:128 * k + 128],
                         wg[:, :], start=i == 0, stop=i == 2, sig=k == NBLK - 1 and i == 2)
        HLm = SM[:, 256:320]
        t = DV(v.tensor_scalar, [t_wp, t_const], HLm[0:64, :], K_[0:64, C_H:C_H + 64], HL[0:64, 0:1], None, ALU.mult)
        wp_v = wpr.rearrange("p (h a n) -> p a h n", a=2, n=128)
        for hh in range(2):
            for i in range(2):
                tp = PE(te.matmul, [t], P[i][64 * hh:64 * hh + 64, :], HLm[0:64, :],
                        wp_v[0:64, hh, 4 * i:4 * i + 4, :], start=True, stop=True, sig=hh == 1 and i == 1)
            t = None
        for i in range(2):
            t_wpo = AC(s.activation, [tp], Wp[:, 512 * i:512 * i + 512], P[i][:, :], ACT.Copy)

        l_ = SM[:, 320:576]
        l3 = l_.rearrange("p (k e) -> p k e", e=8)[:, :, 0:NE]
        p4 = P[4][:, 0:256].rearrange("p (k e) -> p k e", e=8)[:, :, 0:NE]
        im8 = bc(K_[:, C_IM8:C_IM8 + NE], 1, NBLK)
        RW = RW_.rearrange("p (a n) -> p a n", a=4)
        OH = RW[:, 0].rearrange("p (a k e) -> p a k e", a=2, e=8)
        oh_flat = RW[:, 0]
        M12 = SM[:, 576:640].rearrange("p (a k) -> p a k", a=2)
        bi = SM[:, 640:672]
        ew3 = RW[:, 1, 0:256].rearrange("p (k e) -> p k e", e=8)[:, :, 0:NE]
        t_oh0 = DV(v.memset, [], oh_flat, 0.0)
        t = DV(v.tensor_copy, [t_lg], l3, p4)
        t_p4 = t
        for a in range(2):
            tm_ = DV(v.tensor_reduce, [t], M12[:, a], l3, AX, ALU.max)
            t1 = DV(v.tensor_tensor, [tm_], ew3, l3, bc(M12[:, a], 2, NE), ALU.is_ge)
            t1 = DV(v.tensor_tensor, [t1, t_const], ew3, ew3, im8, ALU.mult)
            t1 = DV(v.tensor_reduce, [t1], bi, ew3, AX, ALU.min)
            t1 = DV(v.tensor_tensor, [t1, t_oh0], OH[:, a, :, 0:NE], im8, bc(bi, 2, NE), ALU.is_equal)
            if a == 0:
                t1 = DV(v.tensor_scalar, [t1], ew3, OH[:, 0, :, 0:NE], -1e30, None, ALU.mult)
                t = DV(v.tensor_tensor, [t1], l3, l3, ew3, ALU.add)
        t_oh = t1
        t_cn = PE(te.matmul, [t_oh, t_p5], P[7][:, :], ustr, oh_flat, start=True, stop=True, sig=True)
        t_tt = PE(te.matmul, [t_p5], P[5][:, :], ones, oh_flat, start=True, stop=True, sig=True)
        pf = [RW[:, 1], RW[:, 2]]
        t = DV(v.tensor_copy, [t_tt], pf[0], P[5][:, :])
        cur = 0
        for sh in (1, 2, 4, 8, 16, 32):
            a_, b_ = pf[cur], pf[1 - cur]
            t1 = DV(v.tensor_copy, [t], b_[:, 0:8 * sh], a_[:, 0:8 * sh])
            t = DV(v.tensor_tensor, [t1], b_[:, 8 * sh:512], a_[:, 8 * sh:512], a_[:, 0:512 - 8 * sh], ALU.add)
            cur = 1 - cur
        cnt = pf[cur]
        t = DV(v.tensor_tensor, [t], cnt, cnt, P[5][:, :], ALU.subtract)
        t_p5 = t
        t = DV(v.tensor_tensor, [t, t_cn], cnt, cnt, P[7][:, :], ALU.add)
        t_p7 = t
        t = DV(v.tensor_tensor, [t], cnt, cnt, oh_flat, ALU.mult)
        pos, base, keep, wk = (SM[:, 672 + 64 * i:736 + 64 * i] for i in range(4))
        t_pos = DV(v.tensor_reduce, [t], pos, cnt.rearrange("p (k e) -> p k e", e=8), AX, ALU.add)
        t = DV(v.tensor_tensor, [t_pos], cnt.rearrange("p (k e) -> p k e", e=8),
               oh_flat.rearrange("p (k e) -> p k e", e=8), bc(K_[:, C_I384:C_I384 + 8], 1, 64), ALU.mult)
        t_base = DV(v.tensor_reduce, [t], base, cnt.rearrange("p (k e) -> p k e", e=8), AX, ALU.add)
        t_keep = DV(v.tensor_scalar, [t_pos], keep, pos, float(CAP), None, ALU.is_lt)
        t = DV(v.tensor_scalar, [t_keep], wk, keep, -1e5, 1e5, ALU.mult, ALU.add)
        t = DV(v.tensor_tensor, [t, t_base], wk, wk, base, ALU.add)
        t = DV(v.tensor_tensor, [t, t_pos], wk, wk, pos, ALU.add)
        t_is = DV(v.tensor_copy, [t], idx_s[:, :], wk)
        t = DV(v.tensor_scalar, [t_is], pos, pos, float(CAP - 1), None, ALU.min)
        t = DV(v.tensor_tensor, [t], pos, pos, base, ALU.add)
        t_ig = DV(v.tensor_copy, [t], idx_g[:, :], pos)
        t = DV(v.tensor_tensor, [], SM[:, 928:960], M12[:, 1], M12[:, 0], ALU.subtract)
        t = AC(s.activation, [t, t_p5], SM[:, 928:960], SM[:, 928:960], ACT.Exp)
        t = DV(v.tensor_scalar, [t], SM[:, 960:992], SM[:, 928:960], 1.0, None, ALU.add)
        t = DV(v.reciprocal, [t], SM[:, 960:992], SM[:, 960:992])
        t1 = DV(v.tensor_tensor, [t], SM[:, 928:960], SM[:, 928:960], SM[:, 960:992], ALU.mult)
        t = DV(v.tensor_tensor, [t1, t_keep], gk[:, 0:32], SM[:, 960:992], keep[:, 0:32], ALU.mult)
        t_gk = DV(v.tensor_tensor, [t1, t_keep], gk[:, 32:64], SM[:, 928:960], keep[:, 32:64], ALU.mult)

        for c in range(64):
            k = c % 32
            t_sc = POD(s_sc, g.indirect_dma_start, [t_is, zt, t_h[k // NB]], xe_d[:, :],
                       bass.IndirectOffsetOnAxis(ap=idx_s[:, c:c + 1], axis=0),
                       h_[:, 128 * k:128 * k + 128], None, bounds_check=NE * SLOT - 1, oob_is_err=False)

        z1, na, u_, w_ = (RW[:, 3, 0:256], RW[:, 3, 256:512], RW[:, 1, 0:256], RW[:, 1, 256:512])
        w2_, q_ = RW[:, 2, 0:256], RW[:, 2, 256:512]
        t = DV(v.tensor_scalar, [t_z, t_ig], z1, P[6][:, 0:256], 6.906768, None, ALU.add)
        t_p6 = t
        t1 = DV(v.tensor_scalar, [t], na, z1, -1.0, None, ALU.mult)
        t1 = DV(v.tensor_tensor, [t1], na, z1, na, ALU.min)
        t1 = AC(s.activation, [t1], u_, na, ACT.Exp)
        t1 = DV(v.tensor_scalar, [t1], w_, u_, 2.0, None, ALU.add)
        t1 = DV(v.reciprocal, [t1], w_, w_)
        t1 = DV(v.tensor_tensor, [t1], w_, w_, u_, ALU.mult)
        t1 = DV(v.tensor_tensor, [t1], w2_, w_, w_, ALU.mult)
        t1 = DV(v.tensor_scalar, [t1], q_, w2_, 1.0 / 19, None, ALU.mult)
        for n in (17, 15, 13, 11, 9, 7, 5, 3):
            t1 = DV(v.scalar_tensor_tensor, [t1], q_, q_, 1.0 / n, w2_, ALU.add, ALU.mult)
        t1 = DV(v.scalar_tensor_tensor, [t1], q_, q_, 1.0, w_, ALU.add, ALU.mult)
        t1 = DV(v.tensor_scalar, [t1], z1, z1, 0.0, None, ALU.min)
        t1 = DV(v.scalar_tensor_tensor, [t1], z1, q_, -2.0, z1, ALU.mult, ALU.add)
        t_cs = PE(te.matmul, [t1, t_p4], P[4][:, 0:256], utri, z1, start=True, stop=True, sig=True)
        t_ct = PE(te.matmul, [t1, t_p6], P[6][:, 0:256], ones, z1, start=True, stop=True, sig=True)
        pre = RW[:, 1, 0:256]
        pre4 = pre.rearrange("p (b k h) -> p b k h", b=B, k=NB)
        tot4 = P[6][:, 0:256].rearrange("p (b k h) -> p b k h", b=B, k=NB)
        t = DV(v.memset, [t_ct], pre4[:, :, 0], 0.0)
        for k in range(1, NB):
            t = DV(v.tensor_tensor, [t], pre4[:, :, k], pre4[:, :, k - 1], tot4[:, :, k - 1], ALU.add)
        lG = RW[:, 1, 256:512]
        t_pre = t
        t = DV(v.tensor_tensor, [t, t_cs], lG, P[4][:, 0:256], pre, ALU.add)
        t_lG = t
        lG4 = lG.rearrange("p (b k h) -> p b k h", b=B, k=NB)
        t_ng = DV(v.tensor_scalar, [t_lG], negG[:, :], lG, -1.0, None, ALU.mult)
        es_at = [0, 0, 64, 192]

        def es_view(tile, m):
            return tile[:, es_at[m]:es_at[m] + 64 * m].rearrange("p (b j h) -> p b j h", b=B, h=KVH)
        for m in range(1, 4):
            for j in range(2 * m):
                t = DV(v.tensor_tensor, [t_lG, t_pre], es_view(ES, m)[:, :, j], pre4[:, :, 2 * m], lG4[:, :, j],
                       ALU.subtract)
        t = AC(s.activation, [t], ES[:, :], ES[:, :], ACT.Exp, scale=0.5)
        t1 = DV(v.tensor_scalar, [t], EB[:, :], ES[:, :], GUARD, None, ALU.mult)
        t_es = DV(v.tensor_scalar, [t1], ES[:, :], ES[:, :], 0.125, None, ALU.mult)
        Hc = RW[:, 2, 0:256]
        Hc4 = Hc.rearrange("p (b h k) -> p b h k", b=B, h=KVH)
        t = DV(v.tensor_scalar, [t_lG], Hc4.rearrange("p b h k -> p b k h"), lG4, CLAMP, None, ALU.add)
        for b in range(B):
            for k2 in range(2):
                hv = Hc4[:, b].rearrange("p h (m a) -> p m a h", a=2)[:, :, k2]
                t_hc = DV(v.tensor_tensor, [t], hv, hv, pre4[:, b].rearrange("p (m a) h -> p m a h", a=2)[:, :, 0],
                          ALU.min)
        for i in range(2):
            t = PE(te.transpose, [t_hc, t_p7], P[7][:, 128 * i:128 * i + 128], Hc[:, 128 * i:128 * i + 128], ident,
                   sig=i == 1)
        Hs = RW[:, 3, 0:256]
        t_hs = AC(s.activation, [t], Hs, P[7][:, 0:256], ACT.Copy)
        for i in range(2):
            t_hd = SPD(s_hd, [t_hs], H_d[128 * i:128 * i + 128, :], Hs[:, 128 * i:128 * i + 128])

        bank_free = [[] for _ in range(8)]
        bank_free[0] = bank_free[1] = [t_wpo]
        bank_free[2], bank_free[3] = [last_xt[2]], [last_xt[3]]
        bank_free[4], bank_free[5] = [t_lG], [t_p5]
        bank_free[6], bank_free[7] = [t_pre], [t_hs]
        gt_free = [[t_ht[7], xc_free[0], xc_free[1]], [t_ht[7], t_wq, zt]]
        sil_free, nchunk = [[t_wq], [t_wq]], [0]

        def ups(xT, t_xT, wa, wb, t_wab, n, buf):
            toks = []
            for f in range(4):
                i = nchunk[0] % 2
                nchunk[0] += 1
                pa, pb_ = P[2 * i], P[2 * i + 1]
                ta = PE(te.matmul, t_xT + t_wab + bank_free[2 * i], pa[:, 0:n], wa[:, 128 * f:128 * f + 128], xT,
                        start=True, stop=True, sig=True)
                tb = PE(te.matmul, bank_free[2 * i + 1], pb_[:, 0:n], wb[:, 128 * f:128 * f + 128], xT,
                        start=True, stop=True, sig=True)
                t1 = AC(s.activation, [ta] + sil_free[i], SIL[i][:, 0:n], pa[:, 0:n], ACT.Silu)
                t2 = DV(v.tensor_tensor, [t1, tb] + gt_free[buf], GT[buf][:, 512 * f:512 * f + n], SIL[i][:, 0:n],
                        pb_[:, 0:n], ALU.mult)
                bank_free[2 * i], bank_free[2 * i + 1], sil_free[i] = [t1], [t2], [t2]
                toks.append(t2)
            return toks, tb

        def downs(toks, w2t, nb, buf, bank):
            for q in range(nb):
                for f in range(4):
                    t = PE(te.matmul, [toks[f]] + (bank_free[bank] if q == 0 and f == 0 else []),
                           P[bank][:, 128 * q:128 * q + 128], GT[buf][:, 512 * f + 128 * q:512 * f + 128 * q + 128],
                           w2t[:, 128 * f:128 * f + 128], start=f == 0, stop=f == 3, sig=q == nb - 1 and f == 3)
            gt_free[buf] = [t]
            return t

        def shared_down(gi, toks):
            bank = 4 + gi % 2
            t = downs(toks, W2S, 4, gi % 2, bank)
            o = 512 * gi
            bank_free[bank] = [DV(v.tensor_tensor, [t, t_x[gi // 2]], acc[:, o:o + 512], P[bank][:, :],
                                  acc[:, o:o + 512], ALU.add)]
            return t, bank_free[bank][0]

        prev = None
        for gi in range(8):
            toks, t_up = ups(hT[:, 512 * gi:512 * gi + 512], [t_ht[gi]], W1S, W3S, [t_ws], 512, gi % 2)
            if prev is not None:
                shared_down(gi - 1, prev)
            prev = toks
        t_shared_up = t_up
        _, t_acc = shared_down(7, prev)

        ew_free, xe_free = [[], []], [[], []]
        xet_free, ye_free = [[tp], [tp]], [[tp], [tp]]
        t_ew, t_xe = {}, {}

        def load_expert(e):
            i = e % 2
            w = ew_free[i]
            SPD(s_ew[i], w, EW[i][0], w1[e])
            SPD(s_ew[i], [], EW[i][1], w3[e])
            t_ew[e] = SPD(s_ew[i], [], EW[i][2].rearrange("p (c n) -> p c n", c=4),
                          w2[e].rearrange("(c p) n -> p c n", p=128))

        def load_slots(e):
            i = e % 2
            t_xe[e] = SPD(s_xe[i], [t_sc] + xe_free[i], XE[i].rearrange("p (a c) -> p a c", c=128),
                          xe_d[SLOT * e:SLOT * e + SLOT, :].rearrange("(a p) c -> p a c", p=128))

        def expert_down(e, toks):
            i = e % 2
            bank = 4 + i
            t = downs(toks, EW[i][2], 3, i, bank)
            ew_free[i] = [t]
            ta = AC(s.activation, [t] + ye_free[i], YE[i], P[bank][:, 0:384], ACT.Copy)
            bank_free[bank] = [ta]
            ty = SPD(s_ye, [ta], ye_d[SLOT * e:SLOT * e + SLOT, :].rearrange("(a p) c -> p a c", p=128),
                     YE[i].rearrange("p (a c) -> p a c", c=128))
            ye_free[i] = [ty]
            return ty

        load_expert(0)
        load_expert(1)
        load_slots(0)
        load_slots(1)
        prev = None
        for e in range(NE):
            i = e % 2
            for q in range(3):
                t = PE(te.transpose, [t_xe[e]] + bank_free[6 + i], P[6 + i][:, 128 * q:128 * q + 128],
                       XE[i][:, 128 * q:128 * q + 128], ident, sig=q == 2)
            xe_free[i] = [t]
            t = AC(s.activation, [t] + xet_free[i], XET[i], P[6 + i][:, 0:384], ACT.Copy)
            bank_free[6 + i] = [t]
            toks, t_up = ups(XET[i], [t], EW[i][0], EW[i][1], [t_ew[e]], SLOT, i)
            xet_free[i] = [t_up]
            if prev is not None:
                t_ye = expert_down(e - 1, prev)
                if e + 1 < NE:
                    load_expert(e + 1)
            if e + 2 < NE:
                load_slots(e + 2)
            prev = toks
        t_ye = expert_down(NE - 1, prev)
        ffn_done = [t_es, gt_free[0][0], gt_free[1][0], t_acc, t_ye, t_sc, t_hd, bank_free[4][0], bank_free[5][0],
                    toks[3], bank_free[6][0], bank_free[7][0]]

        yg_free = [[] for _ in range(8)]
        for c in range(64):
            k, a = c // 2, c % 2
            i = c % 8
            ty = POD(s_yg[i], g.indirect_dma_start, [t_ig, t_ye] + yg_free[i], YG[:, 128 * i:128 * i + 128], None,
                     ye_d[:, :], bass.IndirectOffsetOnAxis(ap=idx_g[:, 32 * a + k:32 * a + k + 1], axis=0))
            yg_free[i] = [ty]
            t_acc = DV(v.scalar_tensor_tensor, [ty, t_gk, t_acc], acc[:, 128 * k:128 * k + 128],
                       YG[:, 128 * i:128 * i + 128], gk[:, 32 * a + k:32 * a + k + 1],
                       acc[:, 128 * k:128 * k + 128], ALU.mult, ALU.add)
            yg_free[i] = [t_acc]

        S_BANK, O_BANK = (0, 1, 2), (3, 4)
        s_free, o_free = [ffn_done, ffn_done, ffn_done], [ffn_done, ffn_done]
        gfree = [(5, ffn_done), (6, ffn_done), (7, ffn_done)]
        cos = K_[:, C_COS:C_COS + 512].rearrange("p (k d) -> p k d", k=NB)
        sin = K_[:, C_SIN:C_SIN + 512].rearrange("p (k d) -> p k d", k=NB)
        qk_read, vt_free = [ffn_done, ffn_done], [ffn_done, ffn_done]
        rot_free = [ffn_done, ffn_done]
        t_qk, t_v = {}, {}
        t_one = []
        for i in range(2):
            t_one.append(DV(v.memset, ffn_done, Vt[i].rearrange("p (n d) -> p n d", d=64)[:, :, 63:64], 1.0))

        def project(u, blk):
            b, hu, i = u // 4, u % 4, u % 2
            while not gfree:
                yield
            bank, free = gfree.pop(0)
            o = 1024 * b + 128 * blk
            terms = ((XTh, Wh), (XTh, Wl), (XTl, Wh))
            for n, (xt, w) in enumerate(terms):
                t = PE(te.matmul, [t_xt[2 * b + blk // 4], t_wq] + (free if n == 0 else []), P[bank][:, :],
                       xt[:, o:o + 128], w[:, 512 * hu:512 * hu + 512], start=n == 0, stop=n == 2, sig=n == 2)
            yield
            ri = blk % 2
            qk = QK[i].rearrange("p (k n d) -> p k n d", k=NB, d=64)[:, blk]
            pq = P[bank][:, 0:384].rearrange("p (n d) -> p n d", d=64)
            pr = P[bank][:, 0:384].rearrange("p (n a d) -> p n a d", a=2, d=32)
            rt = ROT[ri].rearrange("p (n a d) -> p n a d", a=2, d=32)
            vt = Vt[i].rearrange("p (k n d) -> p k n d", k=NB, d=64)[:, blk]
            t3 = AC(s.activation, [t, t_one[i]] + vt_free[i], vt[:, :, 0:63],
                    P[bank][:, 384:512].rearrange("p (n d) -> p n d", d=64)[:, :, 0:63], ACT.Copy)
            t1 = DV(v.tensor_tensor, [t, t3] + qk_read[i], qk, pq, bc(cos[:, blk], 1, 6), ALU.mult)
            for a in range(2):
                t2 = DV(v.tensor_tensor, rot_free[ri], rt[:, :, a], pr[:, :, 1 - a],
                        bc(sin[:, blk, 32 * a:32 * a + 32], 1, 6), ALU.mult)
            gfree.append((bank, [t2]))
            yield
            t4 = PO(g.tensor_tensor, [t1, t2], QK[i][:, 384 * blk:384 * blk + 384],
                    QK[i][:, 384 * blk:384 * blk + 384], ROT[ri], ALU.add)
            rot_free[ri] = [t4]
            t_qk[u, blk], t_v[u, blk] = t4, t3

        q_free, k_free, d_free, hr_free = [[], [], []], [[], []], [ffn_done, ffn_done], [ffn_done, ffn_done]
        t_q, t_k, t_d, t_hr = {}, {}, {}, {}

        def pair_parts(p):
            return p // 8, (p % 8), p // 2, p % 2

        def prep_q(p, m):
            b, h, u, hu = pair_parts(p)
            while not gfree or (u, 2 * m + 1) not in t_qk:
                yield
            bank, free = gfree.pop(0)
            qk = QK[u % 2].rearrange("p (k n) -> p k n", k=NB)
            for kb in range(2):
                t = PE(te.transpose, [t_qk[u, 2 * m + kb]] + (free if kb == 0 else []),
                       P[bank][:, 128 * kb:128 * kb + 128], qk[:, 2 * m + kb, 128 * hu:128 * hu + 128], ident,
                       sig=kb == 1)
            qk_read[u % 2] = [t]
            yield
            i = (4 * p + m) % 3
            toks = []
            for hd in range(2):
                src = P[bank][64 * hd:64 * hd + 64, 0:256]
                cols = slice(256 * hd, 256 * hd + 256)
                t1 = AC(s.activation, [t] + q_free[i], Qt[i][0:64, cols], src, ACT.Copy)
                t2 = DV(v.tensor_tensor, [t1], Qt[i][64:128, cols], src, Qt[i][0:64, cols].bitcast(f32),
                        ALU.subtract)
            gfree.append((bank, [t2]))
            t_q[p, m] = [t1, t2]

        def prep_k(p, half):
            b, h, u, hu = pair_parts(p)
            while not gfree or (u, 4 * half + 3) not in t_qk:
                yield
            bank, free = gfree.pop(0)
            qk = QK[u % 2].rearrange("p (k n) -> p k n", k=NB)
            for q in range(4):
                t = PE(te.transpose, [t_qk[u, 4 * half + q]] + (free if q == 0 else []),
                       P[bank][:, 128 * q:128 * q + 128], qk[:, 4 * half + q, 256:384], ident, sig=q == 3)
            qk_read[u % 2] = [t]
            yield
            i = p % 2
            cols = slice(512 * half, 512 * half + 512)
            own, other = slice(64 * hu, 64 * hu + 64), slice(64 - 64 * hu, 128 - 64 * hu)
            t1 = AC(s.activation, [t] + k_free[i], Kh[i][own, cols], P[bank][own, :], ACT.Copy)
            t2 = DV(v.tensor_tensor, [t1] + k_free[i], Kl[i][own, cols], P[bank][own, :],
                    Kh[i][own, cols].bitcast(f32), ALU.subtract)
            gfree.append((bank, [t2]))
            sm = s_k[i][half]
            SPD(sm, [t1], Kh[i][other, cols].bitcast(f32), Kh[i][own, cols].bitcast(f32))
            t_k[p, half] = SPD(sm, [t2], Kl[i][other, cols].bitcast(f32), Kl[i][own, cols].bitcast(f32))

        def load_hrow(p):
            b, h, _, _ = pair_parts(p)
            i = p % 2
            r = (b * KVH + h) * NB
            t_hr[p] = SPD(s_hr[i], [t_hd] + hr_free[i], HR[i],
                          H_d[r:r + NB, :].rearrange("k t -> (k t)").partition_broadcast(128))

        def prep_d(p):
            b, h, _, _ = pair_parts(p)
            i = p % 2
            d3 = D[i].rearrange("p (m n) -> p m n", m=4)
            for m in range(4):
                for k2 in range(2):
                    n = NB * KVH * b + KVH * (2 * m + k2) + h
                    lo, hi = (0, 256) if k2 == 0 else (256, 384)
                    src = HR[i][:, 256 * m + 128 * k2:256 * m + 256]
                    t = AC(s.activation, [t_hr[p], t_ng] + d_free[i], d3[:, m, lo:hi], src, ACT.Exp,
                           bias=negG[:, n:n + 1])
                yield
            hr_free[i] = [t]
            if p + 2 < 32:
                load_hrow(p + 2)
            for lo in (0, 256):
                dv = d3[:, :, lo:lo + 128]
                t_d[p] = PO(g.affine_select, [t], out=dv, in_=dv, pattern=[[0, 4], [1, 128]],
                            compare_op=ALU.is_ge, fill=0.0, base=0, channel_multiplier=-1)

        a_free = [ffn_done] * 6
        run_free, nt_free = [ffn_done, ffn_done], [ffn_done, ffn_done]
        y_free, yt_free, yn_free, y2_free = [ffn_done, ffn_done], [ffn_done, ffn_done], ffn_done, ffn_done
        M_ = [SM[:, 16 * i:16 * i + 16] for i in range(2)]
        sdn, srr, svv, stm, sgg = ([SM[:, 64 + 32 * n + 16 * i:80 + 32 * n + 16 * i] for i in range(2)]
                                   for n in range(5))
        t_y, t_m_, t_pv = {}, {}, {}
        t_last_out = []
        t_yt = {}

        def collect(p, m, t_num, t_run):
            oi = (4 * p + m) % 2
            ob = O_BANK[oi]
            t = AC(s.activation, [t_num] + nt_free[oi], NT[oi], P[ob][:, 0:256], ACT.Copy)
            o_free[oi] = [t]
            yield
            while not gfree:
                yield
            bank, free = gfree.pop(0)
            for q in range(4):
                tm_ = PE(te.transpose, [t_run] + (free if q == 0 else []), P[bank][:, 128 * q:128 * q + 128],
                         RUN[oi][:, 128 * q:128 * q + 128], ident, sig=q == 3)
            run_free[oi] = [tm_]
            yield
            mv = M_[p % 2].rearrange("p (k a) -> p a k", a=2)[:, :, 2 * m:2 * m + 2]
            tr = DV(v.tensor_reduce, [tm_] + (y_free[p % 2] if m == 0 else []), mv,
                    P[bank][:, :].rearrange("p (a k t) -> p a k t", a=2, k=2), AX, ALU.max)
            gfree.append((bank, [tr]))
            t_m_[p, m] = tr
            while not gfree:
                yield
            bank, free = gfree.pop(0)
            for q in range(2):
                ty = PE(te.transpose, [t] + (free if q == 0 else []), P[bank][:, 128 * q:128 * q + 128],
                        NT[oi][:, 128 * q:128 * q + 128], ident, sig=q == 1)
            nt_free[oi] = [ty]
            yield
            t = AC(s.activation, [ty] + (y_free[p % 2] if m == 0 else []), Y[p % 2][:, 256 * m:256 * m + 256],
                   P[bank][:, 0:256], ACT.Copy)
            gfree.append((bank, [t]))
            t_y[p, m] = t

        def finish(p):
            nonlocal yn_free, y2_free, t_acc
            b, h, u, hu = pair_parts(p)
            i = p % 2
            while (p, 3) not in t_y:
                yield
            y3 = Y[i].rearrange("p (n d) -> p n d", d=64)
            yn3 = YN.rearrange("p (n d) -> p n d", d=64)
            y23 = Y2[:, 0:1008].rearrange("p (n d) -> p n d", d=63)
            t = DV(v.scalar_tensor_tensor, [t_m_[p, 3], t_y[p, 3]], sdn[i], M_[i], 1e-6, y3[:, :, 63], ALU.mult, ALU.add)
            t = DV(v.reciprocal, [t], srr[i], sdn[i])
            t_n = DV(v.tensor_tensor, [t] + yn_free, yn3, y3, bc(srr[i], 2, 64), ALU.mult)
            y_free[i] = [t_n]
            yield
            t = AC(s.activation, [t_n] + y2_free, y23, yn3[:, :, 0:63], ACT.Square)
            yield
            t = DV(v.tensor_reduce, [t], svv[i], y23, AX, ALU.add)
            y2_free = [t]
            t = DV(v.tensor_scalar, [t], svv[i], svv[i], 1.0 / 64, 1e-9, ALU.mult, ALU.add)
            yield
            t = rsqrt(svv[i], t, stm[i], sgg[i])
            yield
            t_f = PO(g.tensor_tensor, [t], yn3, yn3, bc(sgg[i], 2, 64), ALU.mult)
            yield
            yield
            for half in range(2):
                while not gfree:
                    yield
                bank, free = gfree.pop(0)
                for q in range(4):
                    o = 512 * half + 128 * q
                    t = PE(te.transpose, [t_f] + (free if q == 0 else []), P[bank][:, 128 * q:128 * q + 128],
                           YN[:, o:o + 128], ident, sig=q == 3)
                yield
                ta = AC(s.activation, [t] + yt_free[i], YT[i][:, 512 * half:512 * half + 512], P[bank][:, :], ACT.Copy)
                gfree.append((bank, [ta]))
            yn_free = [t]
            t_yt[p] = ta
            if hu == 0:
                return
            yield
            for half in range(2):
                while not gfree:
                    yield
                bank, free = gfree.pop(0)
                for q in range(4):
                    o = 512 * half + 128 * q
                    for pp in range(2):
                        t = PE(te.matmul, [t_yt[p - 1], ta] + (free if q + pp == 0 else []),
                               P[bank][:, 128 * q:128 * q + 128], YT[pp][:, o:o + 128],
                               Wp[:, 128 * (h - 1 + pp):128 * (h - 1 + pp) + 128], start=pp == 0, stop=pp == 1,
                               sig=q == 3 and pp == 1)
                yield
                o = 1024 * b + 512 * half
                td = DV(v.tensor_tensor, [t, t_acc], acc[:, o:o + 512], P[bank][:, :], acc[:, o:o + 512], ALU.add)
                t_acc = td
                gfree.append((bank, [td]))
                if h == KVH - 1:
                    t_last_out.append(SPD(s_out, [td], out_v[b, :, 4 * half:4 * half + 4],
                                          acc_v[:, b, 4 * half:4 * half + 4]))
            yt_free[0] = yt_free[1] = [t]

        active = []

        def tick():
            for gen in list(active):
                try:
                    next(gen)
                except StopIteration:
                    active.remove(gen)

        def drain(need):
            while not need():
                assert active
                tick()

        load_hrow(0)
        load_hrow(1)
        for blk in range(NB):
            active.append(project(0, blk))
            tick()
        drain(lambda: not active)
        active += [prep_k(0, 0), prep_k(0, 1), prep_q(0, 0), prep_d(0)]
        drain(lambda: not active)

        steps = [(p, m, j) for p in range(32) for m in range(4) for j in range(2 * m + 2)]
        t_a, t_run, t_qkd = {}, {}, {}
        a_of = {st: n % 6 for n, st in enumerate(steps)}

        def scores(st, n):
            p, m, j = st
            b, h, u, hu = pair_parts(p)
            qi, ki, si = (4 * p + m) % 3, p % 2, n % 3
            last = j == 2 * m + 1
            cols = 256 if last else 512
            rq = Qt[qi][:, :]
            if last:
                rq = rq.rearrange("p (a t) -> p a t", a=2)[:, :, 128:256]
            w = t_q[p, m] + [t_k[p, 0], t_k[p, 1]] + s_free[si]
            PE(te.matmul, w, P[si][:, 0:cols], Kh[ki][:, 128 * j:128 * j + 128], rq, start=True, stop=False)
            t = PE(te.matmul, [], P[si][:, 0:cols], Kl[ki][:, 128 * j:128 * j + 128], rq, start=False, stop=True,
                   sig=True)
            if last:
                q_free[qi] = [t]
                if m == 3:
                    k_free[ki] = [t]
            ai = a_of[st]
            a_ = A[ai]
            if j < 2 * m:
                c = es_at[m] + 16 * m * b + KVH * j + h
                t1 = AC(s.activation, [t, t_es] + a_free[ai], a_, P[si][:, :], ACT.Square, scale=ES[:, c:c + 1],
                        bias=EB[:, c:c + 1])
            else:
                t1 = AC(s.activation, [t] + a_free[ai], a_[:, 0:cols], P[si][:, 0:cols], ACT.Square, scale=0.125)
            s_free[si] = [t1]
            if j >= 2 * m:
                a3 = a_[:, 0:cols].rearrange("p (a t) -> p a t", a=2)
                lo, hi = (256, 384) if last else (0, 256)
                dd = D[ki][:, 384 * m + lo:384 * m + hi]
                t1 = DV(v.scalar_tensor_tensor, [t1, t_d[p]], a3, a3, GUARD * GUARD, bc(dd, 1, 2), ALU.add, ALU.mult)
                if last and m == 3:
                    d_free[ki] = [t1]
            t_a[st] = t1
            ri = (4 * p + m) % 2
            run = RUN[ri]
            r3 = run.rearrange("p (a t) -> p a t", a=2)
            t2 = None
            if j == 1:
                a0 = A[a_of[p, m, 0]]
                if m == 0:
                    a03 = a0.rearrange("p (a t) -> p a t", a=2)
                    DV(v.tensor_copy, [t1] + run_free[ri], r3[:, :, 0:128], a03[:, :, 0:128])
                    t2 = DV(v.tensor_tensor, [], r3[:, :, 128:256], a03[:, :, 128:256],
                            a_[:, 0:256].rearrange("p (a t) -> p a t", a=2), ALU.max)
                else:
                    t2 = DV(v.tensor_tensor, [t1, t_a[p, m, 0]] + run_free[ri], run, a0, a_, ALU.max)
            elif last:
                t2 = DV(v.tensor_tensor, [t1, t_run[p, m]], r3[:, :, 128:256], r3[:, :, 128:256],
                        a_[:, 0:256].rearrange("p (a t) -> p a t", a=2), ALU.max)
            elif j > 1:
                t2 = DV(v.tensor_tensor, [t1, t_run[p, m]], run, run, a_, ALU.max)
            if t2 is not None:
                t_run[p, m] = t2
                t_max[st] = t2
                if j == 1:
                    t_max[p, m, 0] = t2

        t_max = {}

        def values(st):
            p, m, j = st
            b, h, u, hu = pair_parts(p)
            oi = (4 * p + m) % 2
            ob = P[O_BANK[oi]]
            last = j == 2 * m + 1
            ai = a_of[st]
            vt = Vt[u % 2].rearrange("p (k n d) -> p k n d", k=NB, d=64)[:, j, hu]
            for hd in range(2):
                if last:
                    o, r = ob[64 * hd:64 * hd + 64, 128:256], A[ai][:, 128 * hd:128 * hd + 128]
                else:
                    o, r = ob[64 * hd:64 * hd + 64, 0:256], A[ai][:, 256 * hd:256 * hd + 256]
                t = PE(te.matmul, [t_a[st], t_v[u, j]] + (o_free[oi] if j == 0 else []), o, vt, r, start=j == 0,
                       stop=last, sig=hd == 1)
            a_free[ai] = [t, t_max[st]]
            if last:
                if m == 3:
                    if hu == 1:
                        vt_free[u % 2] = [t]
                active.append(collect(p, m, t, t_run[p, m]))
                if m == 3:
                    active.append(finish(p))

        side = []
        for n, st in enumerate(steps):
            p, m, j = st
            u, hu = p // 2, p % 2
            if (m, j) == (0, 0):
                drain(lambda: not side and (p, 0) in t_q and (p, 1) in t_k and p in t_d)
                if p + 1 < 32:
                    if u + 1 < 16:
                        side += [project(u + 1, 4 * hu + blk) for blk in range(4)]
                    side += [prep_d(p + 1), prep_k(p + 1, 0), prep_k(p + 1, 1)]
            if j == 0:
                for i in ((1, 2) if n == 0 else (2,)):
                    if 4 * p + m + i < 128:
                        active.append(prep_q((4 * p + m + i) // 4, (m + i) % 4))
            if side and n % 2 == 0:
                active.append(side.pop(0))
            tick()
            drain(lambda: (p, m) in t_q)
            scores(st, n)
            if n >= LAG:
                values(steps[n - LAG])
        for st in steps[-LAG:]:
            values(st)
        drain(lambda: not active)

        block = ctx.enter_context(nc.Block())

        def play(eng, name):
            seen = {}
            for f, waits, a, k, sm, by in queues[name]:
                for ws, wv in waits:
                    if seen.get(ws.name, 0) < wv:
                        eng.wait_ge(ws, wv)
                        seen[ws.name] = wv
                ins = f(*a, **k)
                if sm is not None:
                    ins.then_inc(sm, by)

        @block.sync
        def _(eng):
            play(eng, "sp")
            for sm, n in ((s_z, 48), (s_hd, 32), (s_ye, 16 * NE), (s_out, 16 * 8), (s_sc, 16 * 64)):
                eng.wait_ge(sm, n)

        @block.tensor
        def _(eng):
            play(eng, "pe")

        @block.scalar
        def _(eng):
            play(eng, "act")

        @block.vector
        def _(eng):
            play(eng, "dve")

        @block.gpsimd
        def _(eng):
            play(eng, "pool")


def constants():
    k = np.zeros((128, NCONST), np.float32)
    i = np.arange(128)
    k[:, C_ID:C_ID + 128] = np.eye(128)
    k[:, C_UT:C_UT + 128] = i[:, None] <= i[None, :]
    k[:, C_US:C_US + 128] = i[:, None] < i[None, :]
    k[:, C_ONE:C_ONE + 128] = 1.0
    hm = np.zeros((64, 64))
    for j in range(63):
        n = j + 1
        hm[:n, j] = 1.0 / math.sqrt(n * (n + 1))
        hm[n, j] = -n / math.sqrt(n * (n + 1))
    k[0:64, C_H:C_H + 64] = hm
    k[64:128, C_H:C_H + 64] = hm
    k[:, C_IM8:C_IM8 + 8] = np.arange(8) - 8
    k[:, C_I384:C_I384 + 8] = np.arange(8) * SLOT
    div = 2.0 * np.pi / float(T) ** (np.arange(0, HD, 2, dtype=np.float32) / HD)
    ang = (np.arange(T, dtype=np.float32)[:, None] * div.astype(np.float32)[None, :]).astype(np.float64)
    cos, sin = (f(ang).astype(np.float32).reshape(NB, 128, 32).transpose(1, 0, 2) for f in (np.cos, np.sin))
    k[:, C_COS:C_COS + 512] = np.concatenate([cos, cos], axis=2).reshape(128, 512)
    k[:, C_SIN:C_SIN + 512] = np.concatenate([-sin, sin], axis=2).reshape(128, 512)
    return k


def kernel(**inputs):
    import concourse.bacc as bacc
    from concourse.bass_utils import run_bass_kernel_spmd

    w = np.asarray(inputs["L0_attn_w_attn"])
    perm = np.concatenate([np.arange(0, HD, 2), np.arange(1, HD, 2)])
    wq = w[:, 0:1024].reshape(C, 16, HD)[:, :, perm].reshape(C, 4, 256)
    wk = w[:, 1024:1536].reshape(C, 8, HD)[:, :, perm].reshape(C, 4, 128)
    arrays = {
        "x": inputs["L0_attn_x"],
        "w_qkv": np.concatenate([wq, wk], axis=2),
        "w_gate": w[:, 2048:2056],
        "wvT": w[:, 1536:2048].reshape(C, 4, 128).transpose(2, 1, 0),
        "w_proj": inputs["L0_attn_w_proj"],
        "ln_w2": np.asarray(inputs["L0_attn_ln_w"]).reshape(HD, 1),
        "ln_g": inputs["L0_ffn_ln_g"],
        "ln_b": inputs["L0_ffn_ln_b"],
        "wr": inputs["L0_ffn_Wr"],
        "w1": inputs["L0_ffn_W1"],
        "w3": inputs["L0_ffn_W3"],
        "w2": inputs["L0_ffn_W2"],
        "w1s": inputs["L0_ffn_W1s"],
        "w3s": inputs["L0_ffn_W3s"],
        "w2s": inputs["L0_ffn_W2s"],
        "const": constants(),
    }
    arrays = {f"in_{n}": np.ascontiguousarray(a) for n, a in arrays.items()}
    nc = bacc.Bacc("TRN2", target_bir_lowering=False, num_devices=1)
    args = [nc.dram_tensor(n, a.shape, mybir.dt.from_np(a.dtype), kind="ExternalInput").ap() for n, a in arrays.items()]
    out = nc.dram_tensor("out_0", (B, T, C), mybir.dt.float32, kind="ExternalOutput").ap()
    block_program(nc, *args, out)
    r = run_bass_kernel_spmd(nc, [arrays], core_ids=[0])
    return r.results[0]["out_0"]
```

```python
import math
from contextlib import ExitStack

import numpy as np

import concourse.bass as bass
from concourse import mybir
from concourse.alu_op_type import AluOpType as ALU

B, T, C = 4, 1024, 128
NB = 8
NBLK = B * NB
KVH = 8
HD = 64
NE = 7
CAP = 366
SLOT = 384
FF = 512
LAG = 3
GUARD = 1e-15
CLAMP = 60.0

C_ID, C_UT, C_US, C_ONE, C_H, C_IM8, C_I384, C_COS, C_SIN = 0, 128, 256, 384, 512, 576, 584, 592, 1104
NCONST = 1616


def block_program(nc, x, w_qkv, w_gate, wvT, w_proj, ln_w2, ln_g, ln_b, wr, w1, w3, w2, w1s, w3s, w2s, const,
                  out):
    f32, f32r, u32, i32 = mybir.dt.float32, mybir.dt.float32r, mybir.dt.uint32, mybir.dt.int32
    ACT = mybir.ActivationFunctionType
    AX = mybir.AxisListType.X
    v, s, te, g = nc.vector, nc.scalar, nc.tensor, nc.gpsimd

    xe_d = nc.dram_tensor("xe_d", (NE * SLOT, C), f32, kind="Internal").ap()
    ye_d = nc.dram_tensor("ye_d", (NE * SLOT, C), f32, kind="Internal").ap()
    H_d = nc.dram_tensor("H_d", (B * KVH * NB, 128), f32, kind="Internal").ap()

    ctx = ExitStack()
    with ctx:
        def sb(name, cols, dt=f32):
            return ctx.enter_context(nc.sbuf_tensor(name, [128, cols], dt))

        def sem(name):
            return ctx.enter_context(nc.semaphore(name))

        queues = {e: [] for e in ("pe", "act", "dve", "pool", "sp")}
        esem = {e: sem("s_" + e) for e in ("pe", "act", "dve", "pool")}
        count = {}

        def put(engine, f, waits, a, k, sm, by):
            waits = [w for w in waits if w is not None]
            queues[engine].append((f, waits, a, k, sm, by))
            if sm is None:
                return None
            count[sm.name] = count.get(sm.name, 0) + by
            return sm, count[sm.name]

        def PE(f, waits, *a, sig=False, **k):
            return put("pe", f, waits, a, k, esem["pe"] if sig else None, 1)

        def AC(f, waits, *a, **k):
            return put("act", f, waits, a, k, esem["act"], 1)

        def DV(f, waits, *a, **k):
            return put("dve", f, waits, a, k, esem["dve"], 1)

        def PO(f, waits, *a, **k):
            return put("pool", f, waits, a, k, esem["pool"], 1)

        def SPD(sm, waits, dst, src):
            return put("sp", nc.sync.dma_start, waits, (dst, src), {}, sm, 16)

        def POD(sm, f, waits, *a, **k):
            return put("pool", f, waits, a, k, sm, 16)

        def bc(ap, axis, n):
            shape = list(ap.shape)
            shape.insert(axis, n)
            return ap.unsqueeze(axis).broadcast_to(shape)

        K_ = sb("consts", NCONST)
        ident, utri, ustr, ones = (K_[:, o:o + 128] for o in (C_ID, C_UT, C_US, C_ONE))
        acc = sb("acc", NBLK * C)
        XTh, XTl = sb("XTh", NBLK * 128, f32r), sb("XTl", NBLK * 128, f32r)
        Wh, Wl = sb("Wh", 2048, f32r), sb("Wl", 2048, f32r)
        Wgh, Wgl = sb("Wgh", 8, f32r), sb("Wgl", 8, f32r)
        Wp = sb("Wp", 1024)
        GB = sb("GB", 2)
        WR = sb("WR", 16)
        negG = sb("negG", 256)
        ES, EB = sb("ES", 384), sb("EB", 384)
        gk = sb("gk", 64)
        idx_s, idx_g = sb("idx_s", 64, u32), sb("idx_g", 64, u32)
        SM = sb("SM", 1024)
        NYG = 4
        YG = sb("YG", NYG * 128)
        Kh = [sb(f"Kh{i}", 1024, f32r) for i in range(2)]
        Kl = [sb(f"Kl{i}", 1024, f32r) for i in range(2)]
        Qt = [sb(f"Qt{i}", 512, f32r) for i in range(3)]
        NU = 25472
        U = sb("U", NU)

        def carve(first):
            at = [first]

            def take(n):
                a = at[0]
                at[0] += n
                assert at[0] <= NU, at
                return U[:, a:a + n]
            return take

        take = carve(0)
        QK = [take(3072) for _ in range(2)]
        ROT = [take(384) for _ in range(2)]
        Vt = [take(1024) for _ in range(2)]
        A = [take(512) for _ in range(6)]
        RUN = [take(512) for _ in range(2)]
        D = [take(384) for _ in range(3)]
        HR = take(1024)
        NT = [take(256) for _ in range(2)]
        Y = [take(1024) for _ in range(2)]
        Y2 = take(1024)
        YT = [take(1024) for _ in range(2)]
        EXPERTS = 20864
        take = carve(EXPERTS)
        EW = [take(512) for _ in range(3)]
        XE, XET, YE = take(384), take(384), take(384)
        GTe = take(1536)
        take = carve(EXPERTS)
        hn = take(4096)
        take = carve(0)
        hT = take(4096)
        XC = [take(1024) for _ in range(2)]
        W32 = take(2048)
        wpr = take(2048)
        wv_ = take(512)
        HL = take(64)
        W1S, W3S, W2S = take(512), take(512), take(512)
        GT = [take(2048) for _ in range(2)]
        SIL = [take(512) for _ in range(2)]
        RW_ = take(2048)
        Z0 = take(896)
        assert 4096 + 2048 + 4096 + 576 + 1536 + 4096 + 1024 + 2048 + 896 <= EXPERTS

        P = [ctx.enter_context(nc.psum_tensor(f"P{i}", [128, 512], f32)) for i in range(8)]

        s_c, s_w, s_hd, s_z, s_sc, s_ye, s_out = (sem(n) for n in ("s_c", "s_w", "s_hd", "s_z", "s_sc", "s_ye",
                                                                    "s_out"))
        s_wp, s_ws = sem("s_wp"), sem("s_ws")
        s_x = [sem(f"s_x{i}") for i in range(4)]
        s_ew, s_xe, s_hr = sem("s_ew"), sem("s_xe"), sem("s_hr")
        s_k = [[sem(f"s_k{i}{n}") for n in range(2)] for i in range(2)]
        s_yg = [sem(f"s_yg{i}") for i in range(NYG)]

        x_v = x.rearrange("b (k p) c -> b p k c", p=128)
        out_v = out.rearrange("b (k p) c -> b p k c", p=128)
        acc_v = acc[:, :].rearrange("p (b k c) -> p b k c", b=B, k=NB)
        t_x = [SPD(s_x[0], [], acc_v[:, 0], x_v[0])]
        t_const = SPD(s_c, [], K_[:, :], const)
        SPD(s_w, [], WR[:, 0:7], wr)
        SPD(s_w, [], WR[:, 8:16], w_gate)
        SPD(s_w, [], GB[:, 0:1], ln_g)
        t_w = SPD(s_w, [], GB[:, 1:2], ln_b)
        t_x.append(SPD(s_x[1], [], acc_v[:, 1], x_v[1]))
        SPD(s_ws, [], W1S, w1s)
        SPD(s_ws, [], W3S, w3s)
        t_ws = SPD(s_ws, [], W2S.rearrange("p (c n) -> p c n", c=4), w2s.rearrange("(c p) n -> p c n", p=128))
        for b in (2, 3):
            t_x.append(SPD(s_x[b], [], acc_v[:, b], x_v[b]))
        SPD(s_wp, [], W32.rearrange("p (u n) -> p u n", u=4)[:, :, 0:384], w_qkv)
        SPD(s_wp, [], wv_.rearrange("p (u n) -> p u n", u=4), wvT)
        SPD(s_wp, [], wpr.rearrange("p (h n) -> p h n", h=16)[0:64], w_proj.rearrange("(h d) n -> d h n", d=64))
        t_wp = SPD(s_wp, [], HL[0:64, 0:1], ln_w2)

        active, now = [], [0]

        def tick():
            now[0] += 1
            for gen in list(active):
                try:
                    next(gen)
                except StopIteration:
                    active.remove(gen)

        def drain(need):
            while not need():
                assert active
                tick()

        def rsqrt(val, t_val, half, tmp, res):
            t = DV(v.tensor_scalar, [t_val], res.bitcast(i32), val.bitcast(i32), -0.5, 1597463007.0, ALU.mult, ALU.add)
            th = DV(v.tensor_scalar, [t_val], half, val, -0.5, None, ALU.mult)
            for n in range(3):
                t = DV(v.tensor_tensor, [t], tmp, res, res, ALU.mult)
                yield
                t = DV(v.tensor_tensor, [t, th], tmp, tmp, half, ALU.mult)
                yield
                t = DV(v.scalar_tensor_tensor, [t], res, tmp, 1.5, res, ALU.add, ALU.mult)
                yield
            return t

        t_m = DV(v.memset, [], Z0, 0.0)
        xe_z = xe_d.rearrange("(a p) c -> p a c", p=128)
        for i in range(3):
            zt = SPD(s_z, [t_m], xe_z[:, 7 * i:7 * i + 7], Z0.rearrange("p (a c) -> p a c", c=128))

        bank_free = [[] for _ in range(8)]
        t_hn, t_xt, t_ht, t_ln = {}, {}, {}, {}
        xc_free = [[], []]
        gate_terms = ((XTh, Wgh), (XTh, Wgl), (XTl, Wgh))

        def norm(b):
            sm = SM[:, 64 * b:64 * b + 64]
            st, mv = sm[:, 0:6], sm[:, 8:24].rearrange("p (k a) -> p k a", a=2)
            var, half, tmp, rs = (sm[:, 24 + 8 * i:32 + 8 * i] for i in range(4))
            st = SM[:, 256 + 48 * b:304 + 48 * b]
            xc = XC[b % 2]
            xin, xout, t_in, free = acc[:, 1024 * b:1024 * b + 1024], xc, [t_x[b]], xc_free[b % 2]
            for layer in range(2):
                for k in range(NB):
                    t = DV(v.bn_stats, t_in, st[:, 6 * k:6 * k + 6], xin[:, 128 * k:128 * k + 128])
                    if k % 4 == 3:
                        yield
                for k in range(NB):
                    t = DV(v.bn_aggr, [t], mv[:, k], st[:, 6 * k:6 * k + 6])
                yield
                t = DV(v.tensor_scalar, [t], var, mv[:, :, 1], 1e-5, None, ALU.add)
                t = yield from rsqrt(var, t, half, tmp, rs)
                for k in range(NB):
                    t = DV(v.tensor_scalar, [t] + free, xout[:, 128 * k:128 * k + 128], xin[:, 128 * k:128 * k + 128],
                           mv[:, k, 0:1], rs[:, k:k + 1], ALU.subtract, ALU.mult)
                    if k % 4 == 3:
                        yield
                if layer == 0:
                    t_n = t
                    active.append(turn_x(b, t))
                    xin, xout, t_in, free = xc, hn[:, 1024 * b:1024 * b + 1024], [t], []
            t_hn[b] = t
            xc_free[b % 2] = [t, t_xt_pe[b]]
            active.append(turn_h(b, t))
            t_ln[b] = t

        t_xt_pe = {}

        def turn_x(b, t_n):
            xc = XC[b % 2]
            for i in range(2):
                o = 1024 * b + 512 * i
                for q in range(4):
                    t = PE(te.transpose, [t_n, t_const] + bank_free[6], P[6][:, 128 * q:128 * q + 128],
                           xc[:, 512 * i + 128 * q:512 * i + 128 * q + 128], ident, sig=q == 3)
                t_xt_pe[b] = t
                ta = AC(s.activation, [t], XTh[:, o:o + 512], P[6][:, :], ACT.Copy)
                bank_free[6] = [DV(v.tensor_tensor, [ta], XTl[:, o:o + 512], P[6][:, :],
                                   XTh[:, o:o + 512].bitcast(f32), ALU.subtract)]
                t_xt[2 * b + i] = bank_free[6][0]
                yield
            for k in range(NB * b, NB * b + NB):
                for i, (xt, wg) in enumerate(gate_terms):
                    t_z[0] = PE(te.matmul, [t_xt[k // 4], t_wg] + bank_free[5], P[5][:, 8 * k:8 * k + 8],
                                xt[:, 128 * k:128 * k + 128], wg[:, :], start=i == 0, stop=i == 2, sig=i == 2)
                if k % 4 == 3:
                    yield
            t_gate[b] = t_z[0]

        def turn_h(b, t_n):
            for i in range(2):
                o = 1024 * b + 512 * i
                for q in range(4):
                    t = PE(te.transpose, [t_n, t_const] + bank_free[7], P[7][:, 128 * q:128 * q + 128],
                           hn[:, o + 128 * q:o + 128 * q + 128], ident, sig=q == 3)
                bank_free[7] = [AC(s.activation, [t, t_w], hT[:, o:o + 512], P[7][:, :], ACT.Identity,
                                   scale=GB[:, 0:1], bias=GB[:, 1:2])]
                t_ht[2 * b + i] = bank_free[7][0]
                yield
            for k in range(NB * b, NB * b + NB):
                t_lg[0] = PE(te.matmul, [t_ht[k // 4]], P[5][:, 256 + 8 * k:256 + 8 * k + 7],
                             hT[:, 128 * k:128 * k + 128], WR[:, 0:7], start=True, stop=True, sig=True)
                if k % 4 == 3:
                    yield
            t_route[b] = t_lg[0]

        t_z, t_lg, t_gate, t_route = [None], [None], {}, {}
        t_g0 = AC(s.activation, [t_w], Wgh[:, :], WR[:, 8:16], ACT.Copy)
        t_wg = DV(v.tensor_tensor, [t_g0], Wgl[:, :], WR[:, 8:16], Wgh[:, :].bitcast(f32), ALU.subtract)

        def weights():
            W4 = W32.rearrange("p (u n) -> p u n", u=4)
            for hh in range(2):
                for u in range(4):
                    t = PE(te.matmul, [t_wp, t_const] + bank_free[6 + hh], P[6 + hh][:, 64 * u:64 * u + 64],
                           wv_[64 * hh:64 * hh + 64, 128 * u:128 * u + 128], K_[64 * hh:64 * hh + 64, C_H:C_H + 64],
                           start=True, stop=True, sig=u == 3)
                t = AC(s.activation, [t], W4[:, :, 384 + 64 * hh:448 + 64 * hh],
                       P[6 + hh][:, 0:256].rearrange("p (u n) -> p u n", u=4), ACT.Copy)
                bank_free[6 + hh] = [t]
            yield
            for i in range(4):
                o = 512 * i
                ta = AC(s.activation, [t], Wh[:, o:o + 512], W32[:, o:o + 512], ACT.Copy)
                yield
                t_wq[0] = DV(v.tensor_tensor, [ta], Wl[:, o:o + 512], W32[:, o:o + 512],
                             Wh[:, o:o + 512].bitcast(f32), ALU.subtract)
                yield
            HLm = SM[:, 448:512]
            t = DV(v.tensor_scalar, [t_wp, t_const], HLm[0:64, :], K_[0:64, C_H:C_H + 64], HL[0:64, 0:1], None,
                   ALU.mult)
            wp_v = wpr.rearrange("p (h a n) -> p a h n", a=2, n=128)
            for i in range(2):
                for hh in range(2):
                    tp = PE(te.matmul, [t] + bank_free[6 + i], P[6 + i][64 * hh:64 * hh + 64, :], HLm[0:64, :],
                            wp_v[0:64, hh, 4 * i:4 * i + 4, :], start=True, stop=True, sig=hh == 1)
                bank_free[6 + i] = [AC(s.activation, [tp], Wp[:, 512 * i:512 * i + 512], P[6 + i][:, :], ACT.Copy)]
                yield
            t_wpe[0] = tp

        t_wq, t_wpe = [None], [None]
        RW = RW_.rearrange("p (a n) -> p a n", a=4)

        es_at = [0, 0, 64, 192]

        def forget():
            z1, na, u_, w_ = (RW[:, 3, 0:256], RW[:, 3, 256:512], RW[:, 1, 0:256], RW[:, 1, 256:512])
            w2_, q_ = RW[:, 2, 0:256], RW[:, 2, 256:512]
            t = DV(v.tensor_scalar, [t_gate[3], t_route[3]], z1, P[5][:, 0:256], 6.906768, None, ALU.add)
            tl = DV(v.tensor_copy, [], RW[:, 0, 0:256].rearrange("p (k e) -> p k e", e=8)[:, :, 0:NE],
                    P[5][:, 256:512].rearrange("p (k e) -> p k e", e=8)[:, :, 0:NE])
            t_logits[0] = tl
            bank_free[5] = [tl]
            yield
            t1 = DV(v.tensor_scalar, [t], na, z1, -1.0, None, ALU.mult)
            t1 = DV(v.tensor_tensor, [t1], na, z1, na, ALU.min)
            t1 = AC(s.activation, [t1], u_, na, ACT.Exp)
            yield
            t1 = DV(v.tensor_scalar, [t1], w_, u_, 2.0, None, ALU.add)
            yield
            t1 = DV(v.reciprocal, [t1], w_, w_)
            yield
            t1 = DV(v.tensor_tensor, [t1], w_, w_, u_, ALU.mult)
            yield
            t1 = DV(v.tensor_tensor, [t1], w2_, w_, w_, ALU.mult)
            yield
            t1 = DV(v.tensor_scalar, [t1], q_, w2_, 1.0 / 19, None, ALU.mult)
            for n in (17, 15, 13, 11, 9, 7, 5, 3):
                yield
                t1 = DV(v.scalar_tensor_tensor, [t1], q_, q_, 1.0 / n, w2_, ALU.add, ALU.mult)
            yield
            t1 = DV(v.scalar_tensor_tensor, [t1], q_, q_, 1.0, w_, ALU.add, ALU.mult)
            t1 = DV(v.tensor_scalar, [t1], z1, z1, 0.0, None, ALU.min)
            t1 = DV(v.scalar_tensor_tensor, [t1], z1, q_, -2.0, z1, ALU.mult, ALU.add)
            t_cs = PE(te.matmul, [t1] + bank_free[5], P[5][:, 0:256], utri, z1, start=True, stop=True, sig=True)
            t_ct = PE(te.matmul, [t1] + bank_free[6], P[6][:, 0:256], ones, z1, start=True, stop=True, sig=True)
            yield
            pre = RW[:, 1, 0:256]
            pre4 = pre.rearrange("p (b k h) -> p b k h", b=B, k=NB)
            tot4 = P[6][:, 0:256].rearrange("p (b k h) -> p b k h", b=B, k=NB)
            t = DV(v.memset, [t_ct], pre4[:, :, 0], 0.0)
            for k in range(1, NB):
                t = DV(v.tensor_tensor, [t], pre4[:, :, k], pre4[:, :, k - 1], tot4[:, :, k - 1], ALU.add)
                yield
            bank_free[6] = [t]
            lG = RW[:, 1, 256:512]
            t_pre = t
            t_lG = DV(v.tensor_tensor, [t, t_cs], lG, P[5][:, 0:256], pre, ALU.add)
            bank_free[5] = [t_lG]
            yield
            lG4 = lG.rearrange("p (b k h) -> p b k h", b=B, k=NB)
            Hc = RW[:, 2, 0:256]
            Hc4 = Hc.rearrange("p (b h k) -> p b h k", b=B, h=KVH)
            t = DV(v.tensor_scalar, [t_lG], Hc4.rearrange("p b h k -> p b k h"), lG4, CLAMP, None, ALU.add)
            yield
            for b in range(B):
                for k2 in range(2):
                    hv = Hc4[:, b].rearrange("p h (m a) -> p m a h", a=2)[:, :, k2]
                    t_hc = DV(v.tensor_tensor, [t], hv, hv,
                              pre4[:, b].rearrange("p (m a) h -> p m a h", a=2)[:, :, 0], ALU.min)
                yield
            for i in range(2):
                t = PE(te.transpose, [t_hc] + bank_free[6], P[6][:, 128 * i:128 * i + 128],
                       Hc[:, 128 * i:128 * i + 128], ident, sig=i == 1)
            Hs = RW[:, 3, 0:256]
            t_hs = AC(s.activation, [t], Hs, P[6][:, 0:256], ACT.Copy)
            bank_free[6] = [t_hs]
            for i in range(2):
                t_hd[0] = SPD(s_hd, [t_hs], H_d[128 * i:128 * i + 128, :], Hs[:, 128 * i:128 * i + 128])
            t_ng[0] = DV(v.tensor_scalar, [t_lG], negG[:, :], lG, -1.0, None, ALU.mult)
            yield
            for m in range(1, 4):
                ev = ES[:, es_at[m]:es_at[m] + 64 * m].rearrange("p (b j h) -> p b j h", b=B, h=KVH)
                for j in range(2 * m):
                    t = DV(v.tensor_tensor, [t_lG, t_pre], ev[:, :, j], pre4[:, :, 2 * m], lG4[:, :, j], ALU.subtract)
                yield
            t = AC(s.activation, [t], ES[:, :], ES[:, :], ACT.Exp, scale=0.5)
            yield
            t1 = DV(v.tensor_scalar, [t], EB[:, :], ES[:, :], GUARD, None, ALU.mult)
            t_es[0] = DV(v.tensor_scalar, [t1], ES[:, :], ES[:, :], 0.125, None, ALU.mult)

        t_logits, t_hd, t_ng, t_es = [None], [None], [None], [None]

        t_is, t_ig, t_gk, t_sc = [None], [None], [None], [None]

        def route():
            while t_es[0] is None:
                yield
            l3 = RW[:, 0, 0:256].rearrange("p (k e) -> p k e", e=8)[:, :, 0:NE]
            im8 = bc(K_[:, C_IM8:C_IM8 + NE], 1, NBLK)
            oh_flat = RW[:, 3]
            OH = oh_flat.rearrange("p (a k e) -> p a k e", a=2, e=8)
            M12 = SM[:, 576:640].rearrange("p (a k) -> p a k", a=2)
            bi = SM[:, 640:672]
            ew3 = RW[:, 0, 256:512].rearrange("p (k e) -> p k e", e=8)[:, :, 0:NE]
            t_oh0 = DV(v.memset, [t_hd[0]], oh_flat, 0.0)
            t = t_logits[0]
            for a in range(2):
                t1 = DV(v.tensor_reduce, [t], M12[:, a], l3, AX, ALU.max)
                yield
                t1 = DV(v.tensor_tensor, [t1], ew3, l3, bc(M12[:, a], 2, NE), ALU.is_ge)
                yield
                t1 = DV(v.tensor_tensor, [t1, t_const], ew3, ew3, im8, ALU.mult)
                yield
                t1 = DV(v.tensor_reduce, [t1], bi, ew3, AX, ALU.min)
                yield
                t1 = DV(v.tensor_tensor, [t1, t_oh0], OH[:, a, :, 0:NE], im8, bc(bi, 2, NE), ALU.is_equal)
                yield
                if a == 0:
                    t1 = DV(v.tensor_scalar, [t1], ew3, OH[:, 0, :, 0:NE], -1e30, None, ALU.mult)
                    yield
                    t = DV(v.tensor_tensor, [t1], l3, l3, ew3, ALU.add)
                    yield
            t_cn = PE(te.matmul, [t1] + bank_free[7], P[7][:, :], ustr, oh_flat, start=True, stop=True, sig=True)
            t_tt = PE(te.matmul, bank_free[5], P[5][:, :], ones, oh_flat, start=True, stop=True, sig=True)
            yield
            pf = [RW[:, 1], RW[:, 2]]
            t = DV(v.tensor_copy, [t_tt], pf[0], P[5][:, :])
            cur = 0
            for sh in (1, 2, 4, 8, 16, 32):
                a_, b_ = pf[cur], pf[1 - cur]
                t1 = DV(v.tensor_copy, [t], b_[:, 0:8 * sh], a_[:, 0:8 * sh])
                t = DV(v.tensor_tensor, [t], b_[:, 8 * sh:512], a_[:, 8 * sh:512], a_[:, 0:512 - 8 * sh], ALU.add)
                yield
                cur = 1 - cur
            cnt = pf[cur]
            cn3 = cnt.rearrange("p (k e) -> p k e", e=8)
            t = DV(v.tensor_tensor, [t], cnt, cnt, P[5][:, :], ALU.subtract)
            bank_free[5] = [t]
            yield
            t = DV(v.tensor_tensor, [t, t_cn], cnt, cnt, P[7][:, :], ALU.add)
            bank_free[7] = [t]
            yield
            t = DV(v.tensor_tensor, [t], cnt, cnt, oh_flat, ALU.mult)
            yield
            pos, base, keep, wk = (SM[:, 672 + 64 * i:736 + 64 * i] for i in range(4))
            t_pos = DV(v.tensor_reduce, [t], pos, cn3, AX, ALU.add)
            t = DV(v.tensor_tensor, [t_pos], cn3, oh_flat.rearrange("p (k e) -> p k e", e=8),
                   bc(K_[:, C_I384:C_I384 + 8], 1, 64), ALU.mult)
            yield
            t_base = DV(v.tensor_reduce, [t], base, cn3, AX, ALU.add)
            t_keep = DV(v.tensor_scalar, [t_pos], keep, pos, float(CAP), None, ALU.is_lt)
            yield
            t = DV(v.tensor_scalar, [t_keep], wk, keep, -1e5, 1e5, ALU.mult, ALU.add)
            yield
            t = DV(v.tensor_tensor, [t, t_base], wk, wk, base, ALU.add)
            yield
            t = DV(v.tensor_tensor, [t, t_pos], wk, wk, pos, ALU.add)
            yield
            t_is[0] = DV(v.tensor_copy, [t], idx_s[:, :], wk)
            for c in range(64):
                k = c % 32
                t_sc[0] = POD(s_sc, g.indirect_dma_start, [t_is[0], zt, t_hn[k // NB]], xe_d[:, :],
                              bass.IndirectOffsetOnAxis(ap=idx_s[:, c:c + 1], axis=0),
                              hn[:, 128 * k:128 * k + 128], None, bounds_check=NE * SLOT - 1, oob_is_err=False)
            t = DV(v.tensor_scalar, [t_is[0]], pos, pos, float(CAP - 1), None, ALU.min)
            yield
            t = DV(v.tensor_tensor, [t], pos, pos, base, ALU.add)
            yield
            t_ig[0] = DV(v.tensor_copy, [t], idx_g[:, :], pos)
            e1, e2 = SM[:, 928:960], SM[:, 960:992]
            t = DV(v.tensor_tensor, [], e1, M12[:, 1], M12[:, 0], ALU.subtract)
            t = AC(s.activation, [t], e1, e1, ACT.Exp)
            yield
            t = DV(v.tensor_scalar, [t], e2, e1, 1.0, None, ALU.add)
            yield
            t = DV(v.reciprocal, [t], e2, e2)
            yield
            t = DV(v.tensor_tensor, [t], e1, e1, e2, ALU.mult)
            yield
            t1 = DV(v.tensor_tensor, [t], gk[:, 0:32], e2, keep[:, 0:32], ALU.mult)
            t_gk[0] = DV(v.tensor_tensor, [t1], gk[:, 32:64], e1, keep[:, 32:64], ALU.mult)

        gt_free, sil_free, nchunk = [[], []], [[], []], [0]
        t_acc = None

        def chunk(gi, f):
            i = nchunk[0] % 2
            nchunk[0] += 1
            xT, buf = hT[:, 512 * gi:512 * gi + 512], gi % 2
            pa, pb_ = P[2 * i], P[2 * i + 1]
            ta = PE(te.matmul, [t_ht[gi], t_ws] + bank_free[2 * i], pa[:, :], W1S[:, 128 * f:128 * f + 128], xT,
                    start=True, stop=True, sig=True)
            tb = PE(te.matmul, bank_free[2 * i + 1], pb_[:, :], W3S[:, 128 * f:128 * f + 128], xT, start=True,
                    stop=True, sig=True)
            t1 = AC(s.activation, [ta] + sil_free[i], SIL[i], pa[:, :], ACT.Silu)
            t2 = DV(v.tensor_tensor, [t1, tb] + gt_free[buf], GT[buf][:, 512 * f:512 * f + 512], SIL[i], pb_[:, :],
                    ALU.mult)
            bank_free[2 * i], bank_free[2 * i + 1], sil_free[i] = [t1], [t2], [t2]
            return t2

        def shared_down(gi, toks, half):
            for q in range(2 * half, 2 * half + 2):
                for f in range(4):
                    t = PE(te.matmul, [toks[f]] + (bank_free[4] if q == 0 and f == 0 else []),
                           P[4][:, 128 * q:128 * q + 128],
                           GT[gi % 2][:, 512 * f + 128 * q:512 * f + 128 * q + 128],
                           W2S[:, 128 * f:128 * f + 128], start=f == 0, stop=f == 3, sig=q == 3 and f == 3)
            if half == 0:
                return None
            gt_free[gi % 2] = [t]
            o = 512 * gi
            t = DV(v.tensor_tensor, [t, t_ln[gi // 2]], acc[:, o:o + 512], P[4][:, :], acc[:, o:o + 512], ALU.add)
            bank_free[4] = [t]
            return t

        started = []
        active.append(norm(0))
        drain(lambda: 1 in t_ht)
        prev = None
        for gi in range(8):
            if gi in (0, 1, 3):
                active.append(norm({0: 1, 1: 2, 3: 3}[gi]))
            if gi == 4:
                active.append(weights())
            drain(lambda: gi in t_ht)
            toks = []
            for f in range(4):
                if 3 in t_gate and 3 in t_route and t_logits[0] is None and not started:
                    started.append(1)
                    active += [forget(), route()]
                toks.append(chunk(gi, f))
                for _ in range(4):
                    tick()
                if prev is not None and f in (1, 2):
                    t_acc = shared_down(gi - 1, prev, f - 1) or t_acc
            prev = toks
        shared_down(7, prev, 0)
        t_acc = shared_down(7, prev, 1)
        drain(lambda: t_gk[0] is not None)
        t_hd, t_ng, t_es = t_hd[0], t_ng[0], t_es[0]
        t_wq = t_wq[0]
        pre_done = [t_es, t_hd, t_ng, t_acc, t_wq, t_wpe[0], t_is[0], t_ig[0],
                    t_gk[0]] + gt_free[0] + gt_free[1] + sil_free[0] + sil_free[1]
        for i in range(8):
            pre_done += bank_free[i]

        NS, AGE = 2, 2
        s_free, o_bank = [pre_done] * NS, {}
        gfree = [(n, pre_done, -AGE) for n in range(NS, 8)]

        def bank_ready():
            return gfree and gfree[0][2] + AGE <= now[0]

        def give(bank, free):
            gfree.append((bank, free, now[0]))

        cos = K_[:, C_COS:C_COS + 512].rearrange("p (k d) -> p k d", k=NB)
        sin = K_[:, C_SIN:C_SIN + 512].rearrange("p (k d) -> p k d", k=NB)
        qk_read = [pre_done, pre_done]
        rot_free = [pre_done, pre_done]
        t_qk, t_v, vt_freed = {}, {}, {-2: pre_done, -1: pre_done}
        t_one = []
        for i in range(2):
            t_one.append(DV(v.memset, pre_done, Vt[i].rearrange("p (n d) -> p n d", d=64)[:, :, 63:64], 1.0))

        def project(u, blk):
            b, hu, i = u // 4, u % 4, u % 2
            while not bank_ready() or u - 2 not in vt_freed:
                yield
            bank, free = gfree.pop(0)[:2]
            o = 1024 * b + 128 * blk
            terms = ((XTh, Wh), (XTh, Wl), (XTl, Wh))
            for n, (xt, w) in enumerate(terms):
                t = PE(te.matmul, [t_xt[2 * b + blk // 4], t_wq] + (free if n == 0 else []), P[bank][:, :],
                       xt[:, o:o + 128], w[:, 512 * hu:512 * hu + 512], start=n == 0, stop=n == 2, sig=n == 2)
            yield
            ri = blk % 2
            qk = QK[i].rearrange("p (k n d) -> p k n d", k=NB, d=64)[:, blk]
            pq = P[bank][:, 0:384].rearrange("p (n d) -> p n d", d=64)
            pr = P[bank][:, 0:384].rearrange("p (n a d) -> p n a d", a=2, d=32)
            rt = ROT[ri].rearrange("p (n a d) -> p n a d", a=2, d=32)
            vt = Vt[i].rearrange("p (k n d) -> p k n d", k=NB, d=64)[:, blk]
            t3 = AC(s.activation, [t, t_one[i]] + vt_freed[u - 2], vt[:, :, 0:63],
                    P[bank][:, 384:512].rearrange("p (n d) -> p n d", d=64)[:, :, 0:63], ACT.Copy)
            yield
            t1 = DV(v.tensor_tensor, [t, t3] + qk_read[i], qk, pq, bc(cos[:, blk], 1, 6), ALU.mult)
            for a in range(2):
                t2 = DV(v.tensor_tensor, rot_free[ri], rt[:, :, a], pr[:, :, 1 - a],
                        bc(sin[:, blk, 32 * a:32 * a + 32], 1, 6), ALU.mult)
            give(bank, [t2])
            yield
            t4 = PO(g.tensor_tensor, [t1, t2], QK[i][:, 384 * blk:384 * blk + 384],
                    QK[i][:, 384 * blk:384 * blk + 384], ROT[ri], ALU.add)
            rot_free[ri] = [t4]
            yield
            yield
            yield
            t_qk[u, blk], t_v[u, blk] = t4, t3

        q_free, k_free, d_free, hr_free = [[], [], []], [[], []], [pre_done] * 3, pre_done
        t_q, t_k, t_d, t_hr = {}, {}, {}, {}

        def pair_parts(p):
            return p // 8, (p % 8), p // 2, p % 2

        def prep_q(p, m):
            b, h, u, hu = pair_parts(p)
            while not bank_ready() or (u, 2 * m + 1) not in t_qk:
                yield
            bank, free = gfree.pop(0)[:2]
            qk = QK[u % 2].rearrange("p (k n) -> p k n", k=NB)
            for kb in range(2):
                t = PE(te.transpose, [t_qk[u, 2 * m + kb]] + (free if kb == 0 else []),
                       P[bank][:, 128 * kb:128 * kb + 128], qk[:, 2 * m + kb, 128 * hu:128 * hu + 128], ident,
                       sig=kb == 1)
            qk_read[u % 2] = [t]
            yield
            i = (4 * p + m) % 3
            src = [P[bank][64 * hd:64 * hd + 64, 0:256] for hd in range(2)]
            t1 = []
            for hd in range(2):
                t1.append(AC(s.activation, [t] + q_free[i], Qt[i][0:64, 256 * hd:256 * hd + 256], src[hd], ACT.Copy))
                yield
            for hd in range(2):
                cols = slice(256 * hd, 256 * hd + 256)
                t2 = DV(v.tensor_tensor, [t1[hd]], Qt[i][64:128, cols], src[hd], Qt[i][0:64, cols].bitcast(f32),
                        ALU.subtract)
            give(bank, [t2])
            t_q[p, m] = t1 + [t2]

        def prep_k(p, half):
            b, h, u, hu = pair_parts(p)
            while not bank_ready() or (u, 4 * half + 3) not in t_qk:
                yield
            bank, free = gfree.pop(0)[:2]
            qk = QK[u % 2].rearrange("p (k n) -> p k n", k=NB)
            for q in range(4):
                t = PE(te.transpose, [t_qk[u, 4 * half + q]] + (free if q == 0 else []),
                       P[bank][:, 128 * q:128 * q + 128], qk[:, 4 * half + q, 256:384], ident, sig=q == 3)
            qk_read[u % 2] = [t]
            yield
            i = p % 2
            cols = slice(512 * half, 512 * half + 512)
            own, other = slice(64 * hu, 64 * hu + 64), slice(64 - 64 * hu, 128 - 64 * hu)
            t1 = AC(s.activation, [t] + k_free[i], Kh[i][own, cols], P[bank][own, :], ACT.Copy)
            yield
            t2 = DV(v.tensor_tensor, [t1] + k_free[i], Kl[i][own, cols], P[bank][own, :],
                    Kh[i][own, cols].bitcast(f32), ALU.subtract)
            give(bank, [t2])
            sm = s_k[i][half]
            SPD(sm, [t1], Kh[i][other, cols].bitcast(f32), Kh[i][own, cols].bitcast(f32))
            t_k[p, half] = SPD(sm, [t2], Kl[i][other, cols].bitcast(f32), Kl[i][own, cols].bitcast(f32))

        def load_hrow(p):
            b, h, _, _ = pair_parts(p)
            r = (b * KVH + h) * NB
            t_hr[p] = SPD(s_hr, [t_hd] + hr_free, HR,
                          H_d[r:r + NB, :].rearrange("k t -> (k t)").partition_broadcast(128))

        def prep_d(p, m):
            nonlocal hr_free
            b, h, _, _ = pair_parts(p)
            i = (4 * p + m) % 3
            for k2 in range(2):
                n = NB * KVH * b + KVH * (2 * m + k2) + h
                lo, hi = (0, 256) if k2 == 0 else (256, 384)
                t = AC(s.activation, [t_hr[p], t_ng] + d_free[i], D[i][:, lo:hi],
                       HR[:, 256 * m + 128 * k2:256 * m + 256], ACT.Exp, bias=negG[:, n:n + 1])
            if m == 3:
                hr_free = [t]
                if p + 1 < 32:
                    load_hrow(p + 1)
            yield
            dv = D[i].rearrange("p (a n) -> p a n", n=128)[:, 0:3:2]
            t_d[p, m] = PO(g.affine_select, [t], out=dv, in_=dv, pattern=[[0, 2], [1, 128]],
                           compare_op=ALU.is_ge, fill=0.0, base=0, channel_multiplier=-1)

        a_free = [pre_done] * 6
        run_free, nt_free = [pre_done, pre_done], [pre_done, pre_done]
        y_freed, y2_free = {-2: pre_done, -1: pre_done}, pre_done
        yt_freed = {-1: pre_done}
        M_ = [SM[:, 16 * i:16 * i + 16] for i in range(2)]
        sdn, srr, svv, shf, stm, sgg = ([SM[:, 64 + 32 * n + 16 * i:80 + 32 * n + 16 * i] for i in range(2)]
                                        for n in range(6))
        t_y, t_m_, t_yt = {}, {}, {}
        out_ready = [0] * B

        def finished(b):
            out_ready[b] += 1
            if out_ready[b] == 2:
                for half in range(2):
                    SPD(s_out, [t_acc], out_v[b, :, 4 * half:4 * half + 4], acc_v[:, b, 4 * half:4 * half + 4])

        def collect_max(p, m, t_run):
            oi = (4 * p + m) % 2
            yield
            while not bank_ready() or p - 2 not in y_freed:
                yield
            bank, free = gfree.pop(0)[:2]
            for q in range(4):
                tm_ = PE(te.transpose, [t_run] + (free if q == 0 else []), P[bank][:, 128 * q:128 * q + 128],
                         RUN[oi][:, 128 * q:128 * q + 128], ident, sig=q == 3)
            run_free[oi] = [tm_]
            run_got.add((p, m))
            yield
            mv = M_[p % 2].rearrange("p (k a) -> p a k", a=2)[:, :, 2 * m:2 * m + 2]
            tr = DV(v.tensor_reduce, [tm_] + (y_freed[p - 2] if m == 0 else []), mv,
                    P[bank][:, :].rearrange("p (a k t) -> p a k t", a=2, k=2), AX, ALU.max)
            give(bank, [tr])
            t_m_[p, m] = tr

        def collect(p, m, t_num):
            oi = (4 * p + m) % 2
            t = AC(s.activation, [t_num] + nt_free[oi], NT[oi], P[o_bank[p, m]][:, 0:256], ACT.Copy)
            give(o_bank[p, m], [t])
            yield
            while not bank_ready() or p - 2 not in y_freed:
                yield
            bank, free = gfree.pop(0)[:2]
            for q in range(2):
                ty = PE(te.transpose, [t] + (free if q == 0 else []), P[bank][:, 128 * q:128 * q + 128],
                        NT[oi][:, 128 * q:128 * q + 128], ident, sig=q == 1)
            nt_free[oi] = [ty]
            yield
            t = AC(s.activation, [ty] + (y_freed[p - 2] if m == 0 else []), Y[p % 2][:, 256 * m:256 * m + 256],
                   P[bank][:, 0:256], ACT.Copy)
            give(bank, [t])
            t_y[p, m] = t

        def finish(p):
            nonlocal y2_free, t_acc
            b, h, u, hu = pair_parts(p)
            i = p % 2
            while (p, 3) not in t_y or (p, 3) not in t_m_:
                yield
            yield
            y3 = Y[i].rearrange("p (n d) -> p n d", d=64)
            y23 = Y2[:, 0:1008].rearrange("p (n d) -> p n d", d=63)
            t = DV(v.scalar_tensor_tensor, [t_m_[p, 3], t_y[p, 3]], sdn[i], M_[i], 1e-6, y3[:, :, 63], ALU.mult, ALU.add)
            yield
            t = DV(v.reciprocal, [t], srr[i], sdn[i])
            yield
            t_n = PO(g.tensor_tensor, [t], y3, y3, bc(srr[i], 2, 64), ALU.mult)
            yield
            yield
            yield
            t = AC(s.activation, [t_n] + y2_free, y23, y3[:, :, 0:63], ACT.Square)
            yield
            t = DV(v.tensor_reduce, [t], svv[i], y23, AX, ALU.add)
            y2_free = [t]
            yield
            t = DV(v.tensor_scalar, [t], svv[i], svv[i], 1.0 / 64, 1e-9, ALU.mult, ALU.add)
            yield
            t = yield from rsqrt(svv[i], t, shf[i], stm[i], sgg[i])
            t_f = PO(g.tensor_tensor, [t], y3, y3, bc(sgg[i], 2, 64), ALU.mult)
            yield
            yield
            yield
            while u - 1 not in yt_freed:
                yield
            for half in range(2):
                while not bank_ready():
                    yield
                bank, free = gfree.pop(0)[:2]
                for q in range(4):
                    o = 512 * half + 128 * q
                    t = PE(te.transpose, [t_f] + (free if q == 0 else []), P[bank][:, 128 * q:128 * q + 128],
                           Y[i][:, o:o + 128], ident, sig=q == 3)
                yield
                ta = AC(s.activation, [t] + yt_freed[u - 1], YT[i][:, 512 * half:512 * half + 512], P[bank][:, :],
                        ACT.Copy)
                give(bank, [ta])
            y_freed[p] = [t]
            t_yt[p] = ta
            if hu == 0:
                return
            yield
            for half in range(2):
                while not bank_ready():
                    yield
                bank, free = gfree.pop(0)[:2]
                for q in range(4):
                    o = 512 * half + 128 * q
                    for pp in range(2):
                        t = PE(te.matmul, [t_yt[p - 1], ta] + (free if q + pp == 0 else []),
                               P[bank][:, 128 * q:128 * q + 128], YT[pp][:, o:o + 128],
                               Wp[:, 128 * (h - 1 + pp):128 * (h - 1 + pp) + 128], start=pp == 0, stop=pp == 1,
                               sig=q == 3 and pp == 1)
                yield
                o = 1024 * b + 512 * half
                t_acc = DV(v.tensor_tensor, [t, t_acc], acc[:, o:o + 512], P[bank][:, :], acc[:, o:o + 512], ALU.add)
                give(bank, [t_acc])
            yt_freed[u] = [t]
            if h == KVH - 1:
                finished(b)

        ye_v = ye_d.rearrange("(e a p) c -> e p a c", e=NE, p=128)
        xe_v = xe_d.rearrange("(e a p) c -> e p a c", e=NE, p=128)

        def experts():
            up_free = down_free = xe_free = xet_free = ye_free = [t_sc[0]] + pre_done
            for e in range(NE):
                SPD(s_ew, up_free, EW[0], w1[e])
                SPD(s_ew, up_free, EW[1], w3[e])
                t_ew = SPD(s_ew, down_free, EW[2].rearrange("p (c n) -> p c n", c=4),
                           w2[e].rearrange("(c p) n -> p c n", p=128))
                t_xe = SPD(s_xe, xe_free, XE.rearrange("p (a c) -> p a c", c=128), xe_v[e])
                for _ in range(6):
                    yield
                while not bank_ready():
                    yield
                bank, free = gfree.pop(0)[:2]
                for q in range(3):
                    t = PE(te.transpose, [t_xe] + (free if q == 0 else []), P[bank][:, 128 * q:128 * q + 128],
                           XE[:, 128 * q:128 * q + 128], ident, sig=q == 2)
                xe_free = [t]
                yield
                t_x = AC(s.activation, [t] + xet_free, XET, P[bank][:, 0:384], ACT.Identity, scale=GB[:, 0:1],
                         bias=GB[:, 1:2])
                give(bank, [t_x])
                yield
                t_s = []
                for n in range(8):
                    w, f = n // 4, n % 4
                    while not bank_ready():
                        yield
                    bank, free = gfree.pop(0)[:2]
                    t = PE(te.matmul, [t_x, t_ew] + free, P[bank][:, 0:384], EW[w][:, 128 * f:128 * f + 128], XET,
                           start=True, stop=True, sig=True)
                    yield
                    gt = GTe[:, 384 * f:384 * f + 384]
                    if w == 0:
                        t_s.append(AC(s.activation, [t] + down_free, gt, P[bank][:, 0:384], ACT.Silu))
                        give(bank, [t_s[f]])
                    else:
                        t_s[f] = DV(v.tensor_tensor, [t, t_s[f]], gt, gt, P[bank][:, 0:384], ALU.mult)
                        give(bank, [t_s[f]])
                up_free = xet_free = [t]
                yield
                while not bank_ready():
                    yield
                bank, free = gfree.pop(0)[:2]
                for q in range(3):
                    for f in range(4):
                        t = PE(te.matmul, [t_s[f]] + (free if q + f == 0 else []), P[bank][:, 128 * q:128 * q + 128],
                               GTe[:, 384 * f + 128 * q:384 * f + 128 * q + 128], EW[2][:, 128 * f:128 * f + 128],
                               start=f == 0, stop=f == 3, sig=q == 2 and f == 3)
                    if q < 2:
                        yield
                down_free = [t]
                yield
                t = AC(s.activation, [t] + ye_free, YE, P[bank][:, 0:384], ACT.Copy)
                give(bank, [t])
                t_ye = SPD(s_ye, [t], ye_v[e], YE.rearrange("p (a c) -> p a c", c=128))
                ye_free = [t_ye]
                yield
            for _ in range(4):
                yield
            active.append(combine(t_ye))

        def combine(t_ye):
            nonlocal t_acc
            yg_free, t_g = [[] for _ in range(NYG)], {}
            order = [(k, c) for k in range(NBLK) for c in (k, k + 32)]
            for n in range(64 + 2):
                if n < 64:
                    k, c = order[n]
                    i = n % NYG
                    t_g[n] = POD(s_yg[i], g.indirect_dma_start, [t_ye, t_ig[0]] + yg_free[i],
                                 YG[:, 128 * i:128 * i + 128], None, ye_d[:, :],
                                 bass.IndirectOffsetOnAxis(ap=idx_g[:, c:c + 1], axis=0))
                if n >= 2:
                    k, c = order[n - 2]
                    i = (n - 2) % NYG
                    a_ = acc[:, 128 * k:128 * k + 128]
                    t_acc = DV(v.scalar_tensor_tensor, [t_g[n - 2], t_gk[0], t_acc], a_, YG[:, 128 * i:128 * i + 128],
                               gk[:, c:c + 1], a_, ALU.mult, ALU.add)
                    yg_free[i] = [t_acc]
                    if c >= 32 and k % NB == NB - 1:
                        finished(k // NB)
                yield
                yield

        load_hrow(0)
        for blk in range(NB):
            active.append(project(0, blk))
            tick()
        drain(lambda: not active)
        active += [prep_k(0, 0), prep_k(0, 1), prep_q(0, 0), prep_d(0, 0)]
        drain(lambda: not active)

        steps = [(p, m, j) for p in range(32) for m in range(4) for j in range(2 * m + 2)]
        t_a, t_run = {}, {}
        a_of = {st: n % 6 for n, st in enumerate(steps)}
        run_got = set()
        t_max = {}

        def before(p, m):
            n = 4 * p + m - 2
            return None if n < 0 else (n // 4, n % 4)

        def scores(st, n):
            p, m, j = st
            b, h, u, hu = pair_parts(p)
            qi, ki, si = (4 * p + m) % 3, p % 2, n % NS
            last = j == 2 * m + 1
            cols = 256 if last else 512
            rq = Qt[qi][:, :]
            if last:
                rq = rq.rearrange("p (a t) -> p a t", a=2)[:, :, 128:256]
            w = t_q[p, m] + [t_k[p, 0], t_k[p, 1]] + s_free[si]
            PE(te.matmul, w, P[si][:, 0:cols], Kh[ki][:, 128 * j:128 * j + 128], rq, start=True, stop=False)
            t = PE(te.matmul, [], P[si][:, 0:cols], Kl[ki][:, 128 * j:128 * j + 128], rq, start=False, stop=True,
                   sig=True)
            if last:
                q_free[qi] = [t]
                if m == 3:
                    k_free[ki] = [t]
            ai = a_of[st]
            a_ = A[ai]
            if j < 2 * m:
                c = es_at[m] + 16 * m * b + KVH * j + h
                t1 = AC(s.activation, [t, t_es] + a_free[ai], a_, P[si][:, :], ACT.Square, scale=ES[:, c:c + 1],
                        bias=EB[:, c:c + 1])
            else:
                t1 = AC(s.activation, [t] + a_free[ai], a_[:, 0:cols], P[si][:, 0:cols], ACT.Square, scale=0.125)
            s_free[si] = [t1]
            if j >= 2 * m:
                a3 = a_[:, 0:cols].rearrange("p (a t) -> p a t", a=2)
                lo, hi = (256, 384) if last else (0, 256)
                dd = D[qi][:, lo:hi]
                t1 = DV(v.scalar_tensor_tensor, [t1, t_d[p, m]], a3, a3, GUARD * GUARD, bc(dd, 1, 2), ALU.add, ALU.mult)
                if last:
                    d_free[qi] = [t1]
            t_a[st] = t1
            ri = (4 * p + m) % 2
            run = RUN[ri]
            r3 = run.rearrange("p (a t) -> p a t", a=2)
            t2 = None
            if j == 1:
                drain(lambda: before(p, m) is None or before(p, m) in run_got)
                a0 = A[a_of[p, m, 0]]
                if m == 0:
                    a03 = a0.rearrange("p (a t) -> p a t", a=2)
                    DV(v.tensor_copy, [t1] + run_free[ri], r3[:, :, 0:128], a03[:, :, 0:128])
                    t2 = DV(v.tensor_tensor, [], r3[:, :, 128:256], a03[:, :, 128:256],
                            a_[:, 0:256].rearrange("p (a t) -> p a t", a=2), ALU.max)
                else:
                    t2 = DV(v.tensor_tensor, [t1, t_a[p, m, 0]] + run_free[ri], run, a0, a_, ALU.max)
            elif last:
                t2 = DV(v.tensor_tensor, [t1, t_run[p, m]], r3[:, :, 128:256], r3[:, :, 128:256],
                        a_[:, 0:256].rearrange("p (a t) -> p a t", a=2), ALU.max)
            elif j > 1:
                t2 = DV(v.tensor_tensor, [t1, t_run[p, m]], run, run, a_, ALU.max)
            if t2 is not None:
                t_run[p, m] = t2
                t_max[st] = t2
                if j == 1:
                    t_max[p, m, 0] = t2
            if last:
                active.append(collect_max(p, m, t2))

        def values(st):
            p, m, j = st
            b, h, u, hu = pair_parts(p)
            last = j == 2 * m + 1
            ai = a_of[st]
            vt = Vt[u % 2].rearrange("p (k n d) -> p k n d", k=NB, d=64)[:, j, hu]
            if j == 0:
                drain(bank_ready)
                o_bank[p, m], free = gfree.pop(0)[:2]
            ob = P[o_bank[p, m]]
            for hd in range(2):
                if last:
                    o, r = ob[64 * hd:64 * hd + 64, 128:256], A[ai][:, 128 * hd:128 * hd + 128]
                else:
                    o, r = ob[64 * hd:64 * hd + 64, 0:256], A[ai][:, 256 * hd:256 * hd + 256]
                t = PE(te.matmul, [t_a[st], t_v[u, j]] + (free if j == 0 else []), o, vt, r, start=j == 0,
                       stop=last, sig=hd == 1)
            a_free[ai] = [t, t_max[st]]
            if last:
                if m == 3 and hu == 1:
                    vt_freed[u] = [t]
                active.append(collect(p, m, t))
                if m == 3:
                    active.append(finish(p))

        side = []
        for n, st in enumerate(steps):
            p, m, j = st
            u, hu = p // 2, p % 2
            if (m, j) == (0, 0):
                if p == 1:
                    active.append(experts())
                drain(lambda: not side and (p, 0) in t_q and (p, 0) in t_k and (p, 1) in t_k)
                if p + 1 < 32:
                    if u + 1 < 16:
                        side += [project(u + 1, 4 * hu + blk) for blk in range(4)]
                    side += [prep_k(p + 1, 0), prep_k(p + 1, 1)]
            if j == 0:
                for i in ((1, 2) if n == 0 else (2,)):
                    ahead = 4 * p + m + i
                    if ahead < 128:
                        active += [prep_d(ahead // 4, ahead % 4), prep_q(ahead // 4, ahead % 4)]
            if side and n % 2 == 0:
                active.append(side.pop(0))
            tick()
            drain(lambda: (p, m) in t_q and (p, m) in t_d)
            scores(st, n)
            if n >= LAG:
                values(steps[n - LAG])
        for st in steps[-LAG:]:
            values(st)
        drain(lambda: not active)

        block = ctx.enter_context(nc.Block())

        def play(eng, name):
            seen = {}
            for f, waits, a, k, sm, by in queues[name]:
                for ws, wv in waits:
                    if seen.get(ws.name, 0) < wv:
                        eng.wait_ge(ws, wv)
                        seen[ws.name] = wv
                ins = f(*a, **k)
                if sm is not None:
                    ins.then_inc(sm, by)

        @block.sync
        def _(eng):
            play(eng, "sp")
            for sm, n in ((s_z, 48), (s_hd, 32), (s_ye, 16 * NE), (s_out, 16 * 8), (s_sc, 16 * 64)):
                eng.wait_ge(sm, n)

        @block.tensor
        def _(eng):
            play(eng, "pe")

        @block.scalar
        def _(eng):
            play(eng, "act")

        @block.vector
        def _(eng):
            play(eng, "dve")

        @block.gpsimd
        def _(eng):
            play(eng, "pool")


def constants():
    k = np.zeros((128, NCONST), np.float32)
    i = np.arange(128)
    k[:, C_ID:C_ID + 128] = np.eye(128)
    k[:, C_UT:C_UT + 128] = i[:, None] <= i[None, :]
    k[:, C_US:C_US + 128] = i[:, None] < i[None, :]
    k[:, C_ONE:C_ONE + 128] = 1.0
    hm = np.zeros((64, 64))
    for j in range(63):
        n = j + 1
        hm[:n, j] = 1.0 / math.sqrt(n * (n + 1))
        hm[n, j] = -n / math.sqrt(n * (n + 1))
    k[0:64, C_H:C_H + 64] = hm
    k[64:128, C_H:C_H + 64] = hm
    k[:, C_IM8:C_IM8 + 8] = np.arange(8) - 8
    k[:, C_I384:C_I384 + 8] = np.arange(8) * SLOT
    div = 2.0 * np.pi / float(T) ** (np.arange(0, HD, 2, dtype=np.float32) / HD)
    ang = (np.arange(T, dtype=np.float32)[:, None] * div.astype(np.float32)[None, :]).astype(np.float64)
    cos, sin = (f(ang).astype(np.float32).reshape(NB, 128, 32).transpose(1, 0, 2) for f in (np.cos, np.sin))
    k[:, C_COS:C_COS + 512] = np.concatenate([cos, cos], axis=2).reshape(128, 512)
    k[:, C_SIN:C_SIN + 512] = np.concatenate([-sin, sin], axis=2).reshape(128, 512)
    return k


def kernel(**inputs):
    import concourse.bacc as bacc
    from concourse.bass_utils import run_bass_kernel_spmd

    w = np.asarray(inputs["L0_attn_w_attn"])
    perm = np.concatenate([np.arange(0, HD, 2), np.arange(1, HD, 2)])
    wq = w[:, 0:1024].reshape(C, 16, HD)[:, :, perm].reshape(C, 4, 256)
    wk = w[:, 1024:1536].reshape(C, 8, HD)[:, :, perm].reshape(C, 4, 128)
    arrays = {
        "x": inputs["L0_attn_x"],
        "w_qkv": np.concatenate([wq, wk], axis=2),
        "w_gate": w[:, 2048:2056],
        "wvT": w[:, 1536:2048].reshape(C, 4, 128).transpose(2, 1, 0),
        "w_proj": inputs["L0_attn_w_proj"],
        "ln_w2": np.asarray(inputs["L0_attn_ln_w"]).reshape(HD, 1),
        "ln_g": np.asarray(inputs["L0_ffn_ln_g"]).reshape(C, 1),
        "ln_b": np.asarray(inputs["L0_ffn_ln_b"]).reshape(C, 1),
        "wr": inputs["L0_ffn_Wr"],
        "w1": inputs["L0_ffn_W1"],
        "w3": inputs["L0_ffn_W3"],
        "w2": inputs["L0_ffn_W2"],
        "w1s": inputs["L0_ffn_W1s"],
        "w3s": inputs["L0_ffn_W3s"],
        "w2s": inputs["L0_ffn_W2s"],
        "const": constants(),
    }
    arrays = {f"in_{n}": np.ascontiguousarray(a) for n, a in arrays.items()}
    nc = bacc.Bacc("TRN2", target_bir_lowering=False, num_devices=1)
    args = [nc.dram_tensor(n, a.shape, mybir.dt.from_np(a.dtype), kind="ExternalInput").ap() for n, a in arrays.items()]
    out = nc.dram_tensor("out_0", (B, T, C), mybir.dt.float32, kind="ExternalOutput").ap()
    block_program(nc, *args, out)
    r = run_bass_kernel_spmd(nc, [arrays], core_ids=[0])
    return r.results[0]["out_0"]
```

```python
import math
from contextlib import ExitStack

import numpy as np

import concourse.bass as bass
from concourse import mybir
from concourse.alu_op_type import AluOpType as ALU

B, T, C = 4, 1024, 128
NB = 8
NBLK = B * NB
KVH = 8
HD = 64
NE = 7
CAP = 366
SLOT = 384
FF = 512
LAG = 4
GUARD = 1e-15
CLAMP = 60.0

C_ID, C_UT, C_US, C_ONE, C_H, C_IM8, C_I384, C_COS, C_SIN = 0, 128, 256, 384, 512, 576, 584, 592, 1104
NCONST = 1616


def block_program(nc, x, w_qkv, w_gate, wvT, w_proj, ln_w2, ln_g, ln_b, wr, w1, w3, w2, w1s, w3s, w2s, const,
                  out):
    f32, f32r, u32, i32 = mybir.dt.float32, mybir.dt.float32r, mybir.dt.uint32, mybir.dt.int32
    ACT = mybir.ActivationFunctionType
    AX = mybir.AxisListType.X
    v, s, te, g = nc.vector, nc.scalar, nc.tensor, nc.gpsimd

    xe_d = nc.dram_tensor("xe_d", (NE * SLOT, C), f32, kind="Internal").ap()
    ye_d = nc.dram_tensor("ye_d", (NE * SLOT, C), f32, kind="Internal").ap()
    k_d = nc.dram_tensor("k_d", (2, 64, T), f32, kind="Internal").ap()
    H_d = nc.dram_tensor("H_d", (B * KVH * NB, 128), f32, kind="Internal").ap()

    ctx = ExitStack()
    with ctx:
        def sb(name, cols, dt=f32):
            return ctx.enter_context(nc.sbuf_tensor(name, [128, cols], dt))

        def sem(name):
            return ctx.enter_context(nc.semaphore(name))

        queues = {e: [] for e in ("pe", "act", "dve", "pool", "sp")}
        esem = {e: sem("s_" + e) for e in ("pe", "act", "dve", "pool")}
        count = {}

        def put(engine, f, waits, a, k, sm, by):
            waits = [w for w in waits if w is not None]
            queues[engine].append((f, waits, a, k, sm, by))
            if sm is None:
                return None
            count[sm.name] = count.get(sm.name, 0) + by
            return sm, count[sm.name]

        def PE(f, waits, *a, sig=False, **k):
            return put("pe", f, waits, a, k, esem["pe"] if sig else None, 1)

        def AC(f, waits, *a, **k):
            return put("act", f, waits, a, k, esem["act"], 1)

        def DV(f, waits, *a, **k):
            return put("dve", f, waits, a, k, esem["dve"], 1)

        def PO(f, waits, *a, **k):
            return put("pool", f, waits, a, k, esem["pool"], 1)

        def SPD(sm, waits, dst, src):
            return put("sp", nc.sync.dma_start, waits, (dst, src), {}, sm, 16)

        def POD(sm, f, waits, *a, **k):
            return put("pool", f, waits, a, k, sm, 16)

        def bc(ap, axis, n):
            shape = list(ap.shape)
            shape.insert(axis, n)
            return ap.unsqueeze(axis).broadcast_to(shape)

        K_ = sb("consts", NCONST)
        ident, utri, ustr, ones = (K_[:, o:o + 128] for o in (C_ID, C_UT, C_US, C_ONE))
        acc = sb("acc", NBLK * C)
        XTh, XTl = sb("XTh", NBLK * 128, f32r), sb("XTl", NBLK * 128, f32r)
        Wh, Wl = sb("Wh", 2048, f32r), sb("Wl", 2048, f32r)
        Wgh, Wgl = sb("Wgh", 8, f32r), sb("Wgl", 8, f32r)
        Wp = sb("Wp", 1024)
        GB = sb("GB", 2)
        WR = sb("WR", 16)
        negG = sb("negG", 256)
        ES, EB = sb("ES", 384), sb("EB", 384)
        gk = sb("gk", 64)
        idx_s, idx_g = sb("idx_s", 64, u32), sb("idx_g", 64, u32)
        SM = sb("SM", 1024)
        NYG = 4
        YG = sb("YG", NYG * 128)
        Kh = [sb(f"Kh{i}", 1024, f32r) for i in range(2)]
        Kl = [sb(f"Kl{i}", 1024, f32r) for i in range(2)]
        Qt = [sb(f"Qt{i}", 512, f32r) for i in range(3)]
        NU, NA = 25472, 7
        U = sb("U", NU)

        def carve(first):
            at = [first]

            def take(n):
                a = at[0]
                at[0] += n
                assert at[0] <= NU, at
                return U[:, a:a + n]
            return take

        take = carve(0)
        QK = [take(3072) for _ in range(2)]
        RAW0, ROT = take(384), take(384)
        Vt = [take(1024) for _ in range(2)]
        A = [take(512) for _ in range(NA)]
        RUN = [take(512) for _ in range(3)]
        D = [take(384) for _ in range(3)]
        NT = take(512)
        Y = [take(1024) for _ in range(2)]
        YT = [take(1024) for _ in range(2)]
        HR = take(1024)
        EXPERTS = 20864
        take = carve(EXPERTS)
        EW = [take(512) for _ in range(3)]
        XE, XET, YE = take(384), take(384), take(384)
        GTe = take(1536)
        take = carve(0)
        W32 = take(2048)
        HL = take(64)
        take = carve(3072)
        RW_ = take(2048)
        wpr = take(1024)
        take = carve(6912)
        XC = [take(1024) for _ in range(2)]
        hT = take(4096)
        W1S, W3S, W2S = take(512), take(512), take(512)
        GT = [take(2048) for _ in range(2)]
        SIL = [take(512) for _ in range(2)]
        Z0 = GT[1][:, 0:896]
        take = carve(EXPERTS)
        hn = take(4096)
        wv_ = take(512)

        P = [ctx.enter_context(nc.psum_tensor(f"P{i}", [128, 512], f32)) for i in range(8)]

        s_c, s_w, s_hd, s_z, s_sc, s_ye, s_out = (sem(n) for n in ("s_c", "s_w", "s_hd", "s_z", "s_sc", "s_ye",
                                                                    "s_out"))
        s_wp, s_ws = sem("s_wp"), sem("s_ws")
        s_x = [sem(f"s_x{i}") for i in range(4)]
        s_ew, s_xe, s_hr = sem("s_ew"), sem("s_xe"), sem("s_hr")
        s_kd = [sem(f"s_kd{i}") for i in range(2)]
        t_kd = [None, None]
        s_k = [[sem(f"s_k{i}{n}") for n in range(2)] for i in range(2)]
        s_yg = [sem(f"s_yg{i}") for i in range(NYG)]

        x_v = x.rearrange("b (k p) c -> b p k c", p=128)
        out_v = out.rearrange("b (k p) c -> b p k c", p=128)
        acc_v = acc[:, :].rearrange("p (b k c) -> p b k c", b=B, k=NB)
        t_x = [SPD(s_x[0], [], acc_v[:, 0], x_v[0])]
        t_const = SPD(s_c, [], K_[:, :], const)
        SPD(s_w, [], WR[:, 0:7], wr)
        SPD(s_w, [], WR[:, 8:16], w_gate)
        SPD(s_w, [], GB[:, 0:1], ln_g)
        t_w = SPD(s_w, [], GB[:, 1:2], ln_b)
        t_x.append(SPD(s_x[1], [], acc_v[:, 1], x_v[1]))
        SPD(s_ws, [], W1S, w1s)
        SPD(s_ws, [], W3S, w3s)
        t_ws = SPD(s_ws, [], W2S.rearrange("p (c n) -> p c n", c=4), w2s.rearrange("(c p) n -> p c n", p=128))
        for b in (2, 3):
            t_x.append(SPD(s_x[b], [], acc_v[:, b], x_v[b]))
        SPD(s_wp, [], W32.rearrange("p (u n) -> p u n", u=4)[:, :, 0:384], w_qkv)
        SPD(s_wp, [], wv_.rearrange("p (u n) -> p u n", u=4), wvT)
        for i in range(2):
            half = slice(64 * i, 64 * i + 64)
            SPD(s_wp, [], wpr.rearrange("p (h n) -> p h n", h=8)[half],
                w_proj[512 * i:512 * i + 512].rearrange("(h d) n -> d h n", d=64))
            t_wp = SPD(s_wp, [], HL[half, 0:1], ln_w2)

        active, now = [], [0]

        def tick():
            now[0] += 1
            for gen in list(active):
                try:
                    next(gen)
                except StopIteration:
                    active.remove(gen)

        def drain(need):
            while not need():
                assert active
                tick()

        def rsqrt(val, t_val, half, tmp, res):
            t = DV(v.tensor_scalar, [t_val], res.bitcast(i32), val.bitcast(i32), -0.5, 1597463007.0, ALU.mult, ALU.add)
            th = DV(v.tensor_scalar, [t_val], half, val, -0.5, None, ALU.mult)
            for n in range(3):
                t = DV(v.tensor_tensor, [t], tmp, res, res, ALU.mult)
                yield
                t = DV(v.tensor_tensor, [t, th], tmp, tmp, half, ALU.mult)
                yield
                t = DV(v.scalar_tensor_tensor, [t], res, tmp, 1.5, res, ALU.add, ALU.mult)
                yield
            return t

        t_m = DV(v.memset, [], Z0, 0.0)
        xe_z = xe_d.rearrange("(a p) c -> p a c", p=128)
        for i in range(3):
            zt = SPD(s_z, [t_m], xe_z[:, 7 * i:7 * i + 7], Z0.rearrange("p (a c) -> p a c", c=128))

        bank_free = [[] for _ in range(8)]
        t_hn, t_xt, t_ht, t_ln = {}, {}, {}, {}
        xc_free = [[], []]
        gate_terms = ((XTh, Wgh), (XTh, Wgl), (XTl, Wgh))

        def norm(b):
            sm = SM[:, 64 * b:64 * b + 64]
            st, mv = sm[:, 0:6], sm[:, 8:24].rearrange("p (k a) -> p k a", a=2)
            var, half, tmp, rs = (sm[:, 24 + 8 * i:32 + 8 * i] for i in range(4))
            st = SM[:, 256 + 48 * b:304 + 48 * b]
            xc = XC[b % 2]
            xin, xout, t_in, free = acc[:, 1024 * b:1024 * b + 1024], xc, [t_x[b]], xc_free[b % 2]
            for layer in range(2):
                for k in range(NB):
                    t = DV(v.bn_stats, t_in, st[:, 6 * k:6 * k + 6], xin[:, 128 * k:128 * k + 128])
                    if k % 4 == 3:
                        yield
                while layer == 0 and b > 1 and b - 2 not in t_ln:
                    yield
                t_s = t
                for k in range(NB):
                    t = DV(v.bn_aggr, [t_s], mv[:, k], st[:, 6 * k:6 * k + 6])
                yield
                t = DV(v.tensor_scalar, [t], var, mv[:, :, 1], 1e-5, None, ALU.add)
                t_r = yield from rsqrt(var, t, half, tmp, rs)
                for k in range(NB):
                    normalise = (DV, v) if layer == 0 or b == 0 else (PO, g)
                    t = normalise[0](normalise[1].tensor_scalar, [t_r] + free, xout[:, 128 * k:128 * k + 128],
                                     xin[:, 128 * k:128 * k + 128], mv[:, k, 0:1], rs[:, k:k + 1], ALU.subtract,
                                     ALU.mult)
                    if k % 4 == 3:
                        yield
                if layer == 0:
                    t_n = t
                    active.append(turn_x(b, t))
                    xin, xout, t_in, free = xc, hn[:, 1024 * b:1024 * b + 1024], [t], []
            t_hn[b] = t
            while 2 * b + 1 not in t_xt:
                yield
            xc_free[b % 2] = [t, t_xt_pe[b]]
            active.append(turn_h(b, t))
            t_ln[b] = t

        t_xt_pe, TURN = {}, 8

        def turn_x(b, t_n):
            xc = XC[b % 2]
            for _ in range(TURN):
                yield
            for i in range(2):
                o = 1024 * b + 512 * i
                for q in range(4):
                    t = PE(te.transpose, [t_n, t_const] + bank_free[6], P[6][:, 128 * q:128 * q + 128],
                           xc[:, 512 * i + 128 * q:512 * i + 128 * q + 128], ident, sig=q == 3)
                t_xt_pe[b] = t
                ta = AC(s.activation, [t], XTh[:, o:o + 512], P[6][:, :], ACT.Copy)
                bank_free[6] = [DV(v.tensor_tensor, [ta], XTl[:, o:o + 512], P[6][:, :],
                                   XTh[:, o:o + 512].bitcast(f32), ALU.subtract)]
                t_xt[2 * b + i] = bank_free[6][0]
                for _ in range(4):
                    yield
            for k in range(NB * b, NB * b + NB):
                for i, (xt, wg) in enumerate(gate_terms):
                    t_z[0] = PE(te.matmul, [t_xt[k // 4], t_wg] + bank_free[5], P[5][:, 8 * k:8 * k + 8],
                                xt[:, 128 * k:128 * k + 128], wg[:, :], start=i == 0, stop=i == 2, sig=i == 2)
                if k % 4 == 3:
                    yield
            t_gate[b] = t_z[0]

        def turn_h(b, t_n):
            for _ in range(TURN):
                yield
            for i in range(2):
                o = 1024 * b + 512 * i
                for q in range(4):
                    t = PE(te.transpose, [t_n, t_const] + bank_free[7], P[7][:, 128 * q:128 * q + 128],
                           hn[:, o + 128 * q:o + 128 * q + 128], ident, sig=q == 3)
                bank_free[7] = [AC(s.activation, [t, t_w], hT[:, o:o + 512], P[7][:, :], ACT.Identity,
                                   scale=GB[:, 0:1], bias=GB[:, 1:2])]
                t_ht[2 * b + i] = bank_free[7][0]
                for _ in range(4):
                    yield
            for k in range(NB * b, NB * b + NB):
                t_lg[0] = PE(te.matmul, [t_ht[k // 4]], P[5][:, 256 + 8 * k:256 + 8 * k + 7],
                             hT[:, 128 * k:128 * k + 128], WR[:, 0:7], start=True, stop=True, sig=True)
                if k % 4 == 3:
                    yield
            t_route[b] = t_lg[0]

        t_z, t_lg, t_gate, t_route = [None], [None], {}, {}
        t_g0 = AC(s.activation, [t_w], Wgh[:, :], WR[:, 8:16], ACT.Copy)
        t_wg = DV(v.tensor_tensor, [t_g0], Wgl[:, :], WR[:, 8:16], Wgh[:, :].bitcast(f32), ALU.subtract)

        def weights():
            W4 = W32.rearrange("p (u n) -> p u n", u=4)
            for hh in range(2):
                for u in range(4):
                    t = PE(te.matmul, [t_wp, t_const] + bank_free[6 + hh], P[6 + hh][:, 64 * u:64 * u + 64],
                           wv_[64 * hh:64 * hh + 64, 128 * u:128 * u + 128], K_[64 * hh:64 * hh + 64, C_H:C_H + 64],
                           start=True, stop=True, sig=u == 3)
                t = AC(s.activation, [t], W4[:, :, 384 + 64 * hh:448 + 64 * hh],
                       P[6 + hh][:, 0:256].rearrange("p (u n) -> p u n", u=4), ACT.Copy)
                bank_free[6 + hh] = [t]
            yield
            for i in range(4):
                o = 512 * i
                ta = AC(s.activation, [t], Wh[:, o:o + 512], W32[:, o:o + 512], ACT.Copy)
                yield
                t_wq[0] = DV(v.tensor_tensor, [ta], Wl[:, o:o + 512], W32[:, o:o + 512],
                             Wh[:, o:o + 512].bitcast(f32), ALU.subtract)
                yield
            HLm = SM[:, 448:512]
            t = DV(v.tensor_scalar, [t_wp, t_const], HLm, K_[:, C_H:C_H + 64], HL[:, 0:1], None, ALU.mult)
            yield
            for _ in range(4):
                yield
            wp_v = wpr.rearrange("p (h a n) -> p a h n", a=2, n=128)
            for i in range(2):
                for hh in range(2):
                    tp = PE(te.matmul, [t] + bank_free[6 + i], P[6 + i][64 * hh:64 * hh + 64, :],
                            HLm[64 * i:64 * i + 64, :], wp_v[64 * i:64 * i + 64, hh], start=True, stop=True,
                            sig=hh == 1)
                bank_free[6 + i] = [AC(s.activation, [tp], Wp[:, 512 * i:512 * i + 512], P[6 + i][:, :], ACT.Copy)]
                yield
            t_wpe[0] = tp

        t_wq, t_wpe = [None], [None]
        RW = RW_.rearrange("p (a n) -> p a n", a=4)

        es_at = [0, 0, 64, 192]

        def forget():
            z1, na, u_, w_ = (RW[:, 3, 0:256], RW[:, 3, 256:512], RW[:, 1, 0:256], RW[:, 1, 256:512])
            w2_, q_ = RW[:, 2, 0:256], RW[:, 2, 256:512]
            t = DV(v.tensor_scalar, [t_gate[3], t_route[3]], z1, P[5][:, 0:256], 6.906768, None, ALU.add)
            tl = DV(v.tensor_copy, [], RW[:, 0, 0:256].rearrange("p (k e) -> p k e", e=8)[:, :, 0:NE],
                    P[5][:, 256:512].rearrange("p (k e) -> p k e", e=8)[:, :, 0:NE])
            t_logits[0] = tl
            bank_free[5] = [tl]
            yield
            t1 = DV(v.tensor_scalar, [t], na, z1, -1.0, None, ALU.mult)
            t1 = DV(v.tensor_tensor, [t1], na, z1, na, ALU.min)
            t1 = AC(s.activation, [t1], u_, na, ACT.Exp)
            yield
            t1 = DV(v.tensor_scalar, [t1], w_, u_, 2.0, None, ALU.add)
            yield
            t1 = DV(v.reciprocal, [t1], w_, w_)
            yield
            t1 = DV(v.tensor_tensor, [t1], w_, w_, u_, ALU.mult)
            yield
            t1 = DV(v.tensor_tensor, [t1], w2_, w_, w_, ALU.mult)
            yield
            t1 = DV(v.tensor_scalar, [t1], q_, w2_, 1.0 / 19, None, ALU.mult)
            for n in (17, 15, 13, 11, 9, 7, 5, 3):
                yield
                t1 = DV(v.scalar_tensor_tensor, [t1], q_, q_, 1.0 / n, w2_, ALU.add, ALU.mult)
            yield
            t1 = DV(v.scalar_tensor_tensor, [t1], q_, q_, 1.0, w_, ALU.add, ALU.mult)
            t1 = DV(v.tensor_scalar, [t1], z1, z1, 0.0, None, ALU.min)
            t1 = DV(v.scalar_tensor_tensor, [t1], z1, q_, -2.0, z1, ALU.mult, ALU.add)
            t_cs = PE(te.matmul, [t1] + bank_free[5], P[5][:, 0:256], utri, z1, start=True, stop=True, sig=True)
            t_ct = PE(te.matmul, [], P[5][:, 256:512], ones, z1, start=True, stop=True, sig=True)
            yield
            yield
            yield
            pre = RW[:, 1, 0:256]
            pre4 = pre.rearrange("p (b k h) -> p b k h", b=B, k=NB)
            tot4 = P[5][:, 256:512].rearrange("p (b k h) -> p b k h", b=B, k=NB)
            t = DV(v.memset, [t_ct], pre4[:, :, 0], 0.0)
            for k in range(1, NB):
                t = DV(v.tensor_tensor, [t], pre4[:, :, k], pre4[:, :, k - 1], tot4[:, :, k - 1], ALU.add)
                yield
            lG = RW[:, 1, 256:512]
            t_pre = t
            t_lG = DV(v.tensor_tensor, [t, t_cs], lG, P[5][:, 0:256], pre, ALU.add)
            bank_free[5] = [t_lG]
            yield
            lG4 = lG.rearrange("p (b k h) -> p b k h", b=B, k=NB)
            Hc = RW[:, 2, 0:256]
            Hc4 = Hc.rearrange("p (b h k) -> p b h k", b=B, h=KVH)
            t = DV(v.tensor_scalar, [t_lG], Hc4.rearrange("p b h k -> p b k h"), lG4, CLAMP, None, ALU.add)
            yield
            for b in range(B):
                for k2 in range(2):
                    hv = Hc4[:, b].rearrange("p h (m a) -> p m a h", a=2)[:, :, k2]
                    t_hc = DV(v.tensor_tensor, [t], hv, hv,
                              pre4[:, b].rearrange("p (m a) h -> p m a h", a=2)[:, :, 0], ALU.min)
                yield
            for i in range(2):
                t = PE(te.transpose, [t_hc] + bank_free[5], P[5][:, 128 * i:128 * i + 128],
                       Hc[:, 128 * i:128 * i + 128], ident, sig=i == 1)
            Hs = RW[:, 3, 0:256]
            yield
            t_hs = AC(s.activation, [t], Hs, P[5][:, 0:256], ACT.Copy)
            bank_free[5] = [t_hs]
            for i in range(2):
                t_hd[0] = SPD(s_hd, [t_hs], H_d[128 * i:128 * i + 128, :], Hs[:, 128 * i:128 * i + 128])
            t_ng[0] = DV(v.tensor_scalar, [t_lG], negG[:, :], lG, -1.0, None, ALU.mult)
            yield
            for m in range(1, 4):
                ev = ES[:, es_at[m]:es_at[m] + 64 * m].rearrange("p (b j h) -> p b j h", b=B, h=KVH)
                for j in range(2 * m):
                    t = DV(v.tensor_tensor, [t_lG, t_pre], ev[:, :, j], pre4[:, :, 2 * m], lG4[:, :, j], ALU.subtract)
                yield
            t = AC(s.activation, [t], ES[:, :], ES[:, :], ACT.Exp, scale=0.5)
            yield
            t1 = DV(v.tensor_scalar, [t], EB[:, :], ES[:, :], GUARD, None, ALU.mult)
            t_es[0] = DV(v.tensor_scalar, [t1], ES[:, :], ES[:, :], 0.125, None, ALU.mult)

        t_logits, t_hd, t_ng, t_es = [None], [None], [None], [None]

        t_is, t_ig, t_gk, t_sc = [None], [None], [None], [None]

        def route():
            while t_es[0] is None:
                yield
            l3 = RW[:, 0, 0:256].rearrange("p (k e) -> p k e", e=8)[:, :, 0:NE]
            im8 = bc(K_[:, C_IM8:C_IM8 + NE], 1, NBLK)
            oh_flat = RW[:, 3]
            OH = oh_flat.rearrange("p (a k e) -> p a k e", a=2, e=8)
            M12 = SM[:, 576:640].rearrange("p (a k) -> p a k", a=2)
            bi = SM[:, 640:672]
            ew3 = RW[:, 0, 256:512].rearrange("p (k e) -> p k e", e=8)[:, :, 0:NE]
            t_oh0 = DV(v.memset, [t_hd[0]], oh_flat, 0.0)
            t = t_logits[0]
            for a in range(2):
                t1 = DV(v.tensor_reduce, [t], M12[:, a], l3, AX, ALU.max)
                yield
                t1 = DV(v.tensor_tensor, [t1], ew3, l3, bc(M12[:, a], 2, NE), ALU.is_ge)
                yield
                t1 = DV(v.tensor_tensor, [t1, t_const], ew3, ew3, im8, ALU.mult)
                yield
                t1 = DV(v.tensor_reduce, [t1], bi, ew3, AX, ALU.min)
                yield
                t1 = DV(v.tensor_tensor, [t1, t_oh0], OH[:, a, :, 0:NE], im8, bc(bi, 2, NE), ALU.is_equal)
                yield
                if a == 0:
                    t1 = DV(v.tensor_scalar, [t1], ew3, OH[:, 0, :, 0:NE], -1e30, None, ALU.mult)
                    yield
                    t = DV(v.tensor_tensor, [t1], l3, l3, ew3, ALU.add)
                    yield
            t_tt = PE(te.matmul, [t1] + bank_free[5], P[5][:, :], ones, oh_flat, start=True, stop=True, sig=True)
            yield
            yield
            pf = [RW[:, 1], RW[:, 2]]
            tot = RW[:, 0]
            t = DV(v.tensor_copy, [t_tt], tot, P[5][:, :])
            t_cn = PE(te.matmul, [t], P[5][:, :], ustr, oh_flat, start=True, stop=True, sig=True)
            yield
            t = DV(v.tensor_copy, [t], pf[0][:, 0:8], tot[:, 0:8])
            t = DV(v.tensor_tensor, [t], pf[0][:, 8:512], tot[:, 8:512], tot[:, 0:504], ALU.add)
            yield
            cur = 0
            for sh in (2, 4, 8, 16, 32):
                a_, b_ = pf[cur], pf[1 - cur]
                t1 = DV(v.tensor_copy, [t], b_[:, 0:8 * sh], a_[:, 0:8 * sh])
                t = DV(v.tensor_tensor, [t], b_[:, 8 * sh:512], a_[:, 8 * sh:512], a_[:, 0:512 - 8 * sh], ALU.add)
                yield
                cur = 1 - cur
            cnt = pf[cur]
            cn3 = cnt.rearrange("p (k e) -> p k e", e=8)
            t = DV(v.tensor_tensor, [t], cnt, cnt, tot, ALU.subtract)
            yield
            t = DV(v.tensor_tensor, [t, t_cn], cnt, cnt, P[5][:, :], ALU.add)
            bank_free[5] = [t]
            yield
            t = DV(v.tensor_tensor, [t], cnt, cnt, oh_flat, ALU.mult)
            yield
            pos, base, keep, wk = (SM[:, 672 + 64 * i:736 + 64 * i] for i in range(4))
            t_pos = DV(v.tensor_reduce, [t], pos, cn3, AX, ALU.add)
            t = DV(v.tensor_tensor, [t_pos], cn3, oh_flat.rearrange("p (k e) -> p k e", e=8),
                   bc(K_[:, C_I384:C_I384 + 8], 1, 64), ALU.mult)
            yield
            t_base = DV(v.tensor_reduce, [t], base, cn3, AX, ALU.add)
            t_keep = DV(v.tensor_scalar, [t_pos], keep, pos, float(CAP), None, ALU.is_lt)
            yield
            t = DV(v.tensor_scalar, [t_keep], wk, keep, -1e5, 1e5, ALU.mult, ALU.add)
            yield
            t = DV(v.tensor_tensor, [t, t_base], wk, wk, base, ALU.add)
            yield
            t = DV(v.tensor_tensor, [t, t_pos], wk, wk, pos, ALU.add)
            yield
            t_is[0] = DV(v.tensor_copy, [t], idx_s[:, :], wk)
            active.append(dispatch())
            t = DV(v.tensor_scalar, [t_is[0]], pos, pos, float(CAP - 1), None, ALU.min)
            yield
            t = DV(v.tensor_tensor, [t], pos, pos, base, ALU.add)
            yield
            t_ig[0] = DV(v.tensor_copy, [t], idx_g[:, :], pos)
            e1, e2 = SM[:, 928:960], SM[:, 960:992]
            t = DV(v.tensor_tensor, [], e1, M12[:, 1], M12[:, 0], ALU.subtract)
            t = AC(s.activation, [t], e1, e1, ACT.Exp)
            yield
            t = DV(v.tensor_scalar, [t], e2, e1, 1.0, None, ALU.add)
            yield
            t = DV(v.reciprocal, [t], e2, e2)
            yield
            t = DV(v.tensor_tensor, [t], e1, e1, e2, ALU.mult)
            yield
            t1 = DV(v.tensor_tensor, [t], gk[:, 0:32], e2, keep[:, 0:32], ALU.mult)
            t_gk[0] = DV(v.tensor_tensor, [t1], gk[:, 32:64], e1, keep[:, 32:64], ALU.mult)
            route_done.extend([t_gk[0], t_ig[0], t_wpe[0]])

        def dispatch():
            for c in range(64):
                k = c % 32
                t = POD(s_sc, g.indirect_dma_start, [t_is[0], zt, t_hn[k // NB]], xe_d[:, :],
                        bass.IndirectOffsetOnAxis(ap=idx_s[:, c:c + 1], axis=0),
                        hn[:, 128 * k:128 * k + 128], None, bounds_check=NE * SLOT - 1, oob_is_err=False)
                yield
                yield
                yield
                yield
            t_sc[0] = t

        gt_free, sil_free, nchunk = [[], [zt]], [[], []], [0]
        t_acc = None

        def chunk(gi, f):
            i = nchunk[0] % 2
            nchunk[0] += 1
            xT = hT[:, 512 * gi:512 * gi + 512]
            pa, pb_ = P[2 * i], P[2 * i + 1]
            ta = PE(te.matmul, [t_ht[gi], t_ws] + bank_free[2 * i], pa[:, :], W1S[:, 128 * f:128 * f + 128], xT,
                    start=True, stop=True, sig=True)
            tb = PE(te.matmul, bank_free[2 * i + 1], pb_[:, :], W3S[:, 128 * f:128 * f + 128], xT, start=True,
                    stop=True, sig=True)
            return gi, f, i, ta, tb

        def gate(gi, f, i, ta, tb):
            buf, pa, pb_ = gi % 2, P[2 * i], P[2 * i + 1]
            t1 = AC(s.activation, [ta] + sil_free[i], SIL[i], pa[:, :], ACT.Silu)
            t2 = DV(v.tensor_tensor, [t1, tb] + gt_free[buf], GT[buf][:, 512 * f:512 * f + 512], SIL[i], pb_[:, :],
                    ALU.mult)
            bank_free[2 * i], bank_free[2 * i + 1], sil_free[i] = [t1], [t2], [t2]
            t_gt[gi, f] = t2

        t_gt = {}

        def shared_down(gi, half):
            for q in range(2 * half, 2 * half + 2):
                for f in range(4):
                    t = PE(te.matmul, [t_gt[gi, f]] + (bank_free[4] if q == 0 and f == 0 else []),
                           P[4][:, 128 * q:128 * q + 128],
                           GT[gi % 2][:, 512 * f + 128 * q:512 * f + 128 * q + 128],
                           W2S[:, 128 * f:128 * f + 128], start=f == 0, stop=f == 3, sig=q == 3 and f == 3)
            if half == 1:
                gt_free[gi % 2] = [t]
            return t

        def shared_add(gi, t):
            o = 512 * gi
            t = DV(v.tensor_tensor, [t, t_ln[gi // 2]], acc[:, o:o + 512], P[4][:, :], acc[:, o:o + 512], ALU.add)
            bank_free[4] = [t]
            return t

        NS, AGE = 2, 2
        early_done, route_done, ffn_done = [], [], []
        s_free, o_bank = [ffn_done] * NS, {}
        gfree = []

        def bank_ready():
            return gfree and gfree[0][2] + AGE <= now[0]

        def give(bank, free):
            gfree.append((bank, free, now[0]))

        cos = K_[:, C_COS:C_COS + 512].rearrange("p (k d) -> p k d", k=NB)
        sin = K_[:, C_SIN:C_SIN + 512].rearrange("p (k d) -> p k d", k=NB)
        qk_read = [early_done, route_done]
        RAW = [RAW0, K_[:, C_UT:C_ONE + 128]]
        raw_free, raw_busy, rot_free = [[], route_done], [False, False], [None]
        t_qk, t_v, vt_freed = {}, {}, {-2: early_done, -1: early_done}
        t_one = []

        def project(u, blk):
            b, hu, i = u // 4, u % 4, u % 2
            while not bank_ready() or u - 2 not in vt_freed or (u == 1 and not route_done):
                yield
            bank, free = gfree.pop(0)[:2]
            o = 1024 * b + 128 * blk
            terms = ((XTh, Wh), (XTh, Wl), (XTl, Wh))
            for n, (xt, w) in enumerate(terms):
                t = PE(te.matmul, [t_xt[2 * b + blk // 4], t_wq[0]] + (free if n == 0 else []), P[bank][:, :],
                       xt[:, o:o + 128], w[:, 512 * hu:512 * hu + 512], start=n == 0, stop=n == 2, sig=n == 2)
            yield
            qk = QK[i].rearrange("p (k n d) -> p k n d", k=NB, d=64)[:, blk]
            ri = blk % 2 if u > 0 else 0
            raw = RAW[ri].rearrange("p (n a d) -> p n a d", a=2, d=32)
            rot = ROT.rearrange("p (n a d) -> p n a d", a=2, d=32)
            vt = Vt[i].rearrange("p (k n d) -> p k n d", k=NB, d=64)[:, blk]
            while raw_busy[ri]:
                yield
            raw_busy[ri] = True
            AC(s.activation, [t] + raw_free[ri], RAW[ri], P[bank][:, 0:384], ACT.Copy)
            t3 = AC(s.activation, [t_one[i]] + vt_freed[u - 2], vt[:, :, 0:63],
                    P[bank][:, 384:512].rearrange("p (n d) -> p n d", d=64)[:, :, 0:63], ACT.Copy)
            yield
            t1 = DV(v.tensor_tensor, [t, t3] + qk_read[i], qk, P[bank][:, 0:384].rearrange("p (n d) -> p n d", d=64),
                    bc(cos[:, blk], 1, 6), ALU.mult)
            give(bank, [t1])
            for a in range(2):
                t2 = PO(g.tensor_tensor, [t3, rot_free[0]], rot[:, :, a], raw[:, :, 1 - a],
                        bc(sin[:, blk, 32 * a:32 * a + 32], 1, 6), ALU.mult)
            raw_free[ri] = [t2]
            raw_busy[ri] = False
            t4 = PO(g.tensor_tensor, [t1, t2], QK[i][:, 384 * blk:384 * blk + 384],
                    QK[i][:, 384 * blk:384 * blk + 384], ROT, ALU.add)
            rot_free[0] = t4
            yield
            yield
            yield
            yield
            t_qk[u, blk], t_v[u, blk] = t4, t3

        q_free, k_free, d_free, hr_free = [[], [], []], [[], []], [ffn_done] * 3, []
        t_q, t_k, t_d, t_hr = {}, {}, {}, {}

        def pair_parts(p):
            return p // 8, (p % 8), p // 2, p % 2

        def prep_q(p, m):
            b, h, u, hu = pair_parts(p)
            while not bank_ready() or (u, 2 * m + 1) not in t_qk:
                yield
            bank, free = gfree.pop(0)[:2]
            qk = QK[u % 2].rearrange("p (k n) -> p k n", k=NB)
            for kb in range(2):
                t = PE(te.transpose, [t_qk[u, 2 * m + kb]] + (free if kb == 0 else []),
                       P[bank][:, 128 * kb:128 * kb + 128], qk[:, 2 * m + kb, 128 * hu:128 * hu + 128], ident,
                       sig=kb == 1)
            qk_read[u % 2] = [t]
            yield
            i = (4 * p + m) % 3
            src = [P[bank][64 * hd:64 * hd + 64, 0:256] for hd in range(2)]
            t1 = []
            for hd in range(2):
                t1.append(AC(s.activation, [t] + q_free[i], Qt[i][0:64, 256 * hd:256 * hd + 256], src[hd], ACT.Copy))
                yield
            for hd in range(2):
                cols = slice(256 * hd, 256 * hd + 256)
                t2 = DV(v.tensor_tensor, [t1[hd]], Qt[i][64:128, cols], src[hd], Qt[i][0:64, cols].bitcast(f32),
                        ALU.subtract)
            give(bank, [t2])
            t_q[p, m] = t1 + [t2]

        def prep_k(p, half):
            b, h, u, hu = pair_parts(p)
            while not bank_ready() or (u, 4 * half + 3) not in t_qk:
                yield
            bank, free = gfree.pop(0)[:2]
            qk = QK[u % 2].rearrange("p (k n) -> p k n", k=NB)
            for q in range(4):
                t = PE(te.transpose, [t_qk[u, 4 * half + q]] + (free if q == 0 else []),
                       P[bank][:, 128 * q:128 * q + 128], qk[:, 4 * half + q, 256:384], ident, sig=q == 3)
            qk_read[u % 2] = [t]
            yield
            cols = slice(512 * half, 512 * half + 512)
            t1 = AC(s.activation, [t] + k_free[0], Kh[0][:, cols], P[bank][:, :], ACT.Copy)
            yield
            t2 = DV(v.tensor_tensor, [t1], Kl[0][:, cols], P[bank][:, :], Kh[0][:, cols].bitcast(f32), ALU.subtract)
            give(bank, [t2])
            yield
            parts = ((Kh[0], t1), (Kl[0], t2))
            for n, (kt, tk) in enumerate(parts):
                t_kd[half] = SPD(s_kd[half], [tk, t_k.get((p - 1, 0))], k_d[n, :, cols], kt[64:128, cols].bitcast(f32))
            yield
            for kt, tk in parts:
                t_k[p, half] = SPD(s_k[0][half], [t_kd[half]], kt[64:128, cols].bitcast(f32), kt[0:64, cols].bitcast(f32))

        def load_k(p):
            for n, kt in enumerate((Kh[1], Kl[1])):
                for rows in (slice(0, 64), slice(64, 128)):
                    t = SPD(s_k[1][0], k_free[1] + t_kd, kt[rows, :].bitcast(f32), k_d[n])
            t_k[p, 0] = t_k[p, 1] = t
            yield

        def load_hrow(p):
            b, h, _, _ = pair_parts(p)
            r = (b * KVH + h) * NB
            t_hr[p] = SPD(s_hr, [t_hd[0]] + hr_free, HR,
                          H_d[r:r + NB, :].rearrange("k t -> (k t)").partition_broadcast(128))

        def prep_d(p, m):
            nonlocal hr_free
            b, h, _, _ = pair_parts(p)
            i = (4 * p + m) % 3
            for _ in range(6):
                yield
            for k2 in range(2):
                n = NB * KVH * b + KVH * (2 * m + k2) + h
                lo, hi = (0, 256) if k2 == 0 else (256, 384)
                t = AC(s.activation, [t_hr[p], t_ng[0]] + d_free[i], D[i][:, lo:hi],
                       HR[:, 256 * m + 128 * k2:256 * m + 256], ACT.Exp, bias=negG[:, n:n + 1])
            if m == 3:
                hr_free = [t]
                if p + 1 < 32:
                    load_hrow(p + 1)
            yield
            dv = D[i].rearrange("p (a n) -> p a n", n=128)[:, 0:3:2]
            t_d[p, m] = PO(g.affine_select, [t], out=dv, in_=dv, pattern=[[0, 2], [1, 128]],
                           compare_op=ALU.is_ge, fill=0.0, base=0, channel_multiplier=-1)

        a_free = [ffn_done] * NA
        run_free, nt_free, nt_full = [ffn_done] * 3, [ffn_done], [False]
        y_freed = {-2: ffn_done, -1: ffn_done}
        yt_freed = {-1: ffn_done}
        M_ = [SM[:, 16 * i:16 * i + 16] for i in range(2)]
        sdn, srr, svv, shf, stm, sgg = ([SM[:, 64 + 32 * n + 16 * i:80 + 32 * n + 16 * i] for i in range(2)]
                                        for n in range(6))
        t_y, t_m_, t_yt = {}, {}, {}
        out_ready = [0] * B

        def finished(b):
            out_ready[b] += 1
            if out_ready[b] == 2:
                for half in range(2):
                    SPD(s_out, [t_acc], out_v[b, :, 4 * half:4 * half + 4], acc_v[:, b, 4 * half:4 * half + 4])

        def collect_max(p, m, t_run):
            ri = (4 * p + m) % 3
            for _ in range(3):
                yield
            while not bank_ready() or p - 2 not in y_freed:
                yield
            bank, free = gfree.pop(0)[:2]
            for q in range(4):
                tm_ = PE(te.transpose, [t_run] + (free if q == 0 else []), P[bank][:, 128 * q:128 * q + 128],
                         RUN[ri][:, 128 * q:128 * q + 128], ident, sig=q == 3)
            run_free[ri] = [tm_]
            run_got.add((p, m))
            yield
            mv = M_[p % 2].rearrange("p (k a) -> p a k", a=2)[:, :, 2 * m:2 * m + 2]
            tr = DV(v.tensor_reduce, [tm_] + (y_freed[p - 2] if m == 0 else []), mv,
                    P[bank][:, :].rearrange("p (a k t) -> p a k t", a=2, k=2), AX, ALU.max)
            give(bank, [tr])
            t_m_[p, m] = tr

        def collect(p, m, t_num):
            while nt_full[0] != (m % 2 == 1):
                yield
            nt_full[0] = True
            t = AC(s.activation, [t_num] + nt_free[0], NT[:, 256 * (m % 2):256 * (m % 2) + 256],
                   P[o_bank[p, m]][:, 0:256], ACT.Copy)
            give(o_bank[p, m], [t])
            if m % 2 == 0:
                return
            for _ in range(2):
                yield
            while not bank_ready() or p - 2 not in y_freed:
                yield
            bank, free = gfree.pop(0)[:2]
            for q in range(4):
                ty = PE(te.transpose, [t] + (free if q == 0 else []), P[bank][:, 128 * q:128 * q + 128],
                        NT[:, 128 * q:128 * q + 128], ident, sig=q == 3)
            nt_free[0], nt_full[0] = [ty], False
            yield
            t = AC(s.activation, [ty] + (y_freed[p - 2] if m == 1 else []),
                   Y[p % 2][:, 256 * m - 256:256 * m + 256], P[bank][:, :], ACT.Copy)
            give(bank, [t])
            t_y[p, m] = t

        def finish(p):
            nonlocal t_acc
            b, h, u, hu = pair_parts(p)
            i = p % 2
            while (p, 3) not in t_y or (p, 3) not in t_m_:
                yield
            yield
            y3 = Y[i].rearrange("p (n d) -> p n d", d=64)
            y23 = YT[i][:, 0:1008].rearrange("p (n d) -> p n d", d=63)
            t = DV(v.scalar_tensor_tensor, [t_m_[p, 3], t_y[p, 3]], sdn[i], M_[i], 1e-6, y3[:, :, 63], ALU.mult, ALU.add)
            yield
            t = DV(v.reciprocal, [t], srr[i], sdn[i])
            yield
            t_n = PO(g.tensor_tensor, [t], y3, y3, bc(srr[i], 2, 64), ALU.mult)
            yield
            yield
            yield
            while u - 1 not in yt_freed:
                yield
            t = AC(s.activation, [t_n] + yt_freed[u - 1], y23, y3[:, :, 0:63], ACT.Square)
            yield
            t = DV(v.tensor_reduce, [t], svv[i], y23, AX, ALU.add)
            t_sq = t
            yield
            t = DV(v.tensor_scalar, [t], svv[i], svv[i], 1.0 / 64, 1e-9, ALU.mult, ALU.add)
            yield
            t = yield from rsqrt(svv[i], t, shf[i], stm[i], sgg[i])
            t_f = PO(g.tensor_tensor, [t], y3, y3, bc(sgg[i], 2, 64), ALU.mult)
            yield
            yield
            yield
            for half in range(2):
                while not bank_ready():
                    yield
                bank, free = gfree.pop(0)[:2]
                for q in range(4):
                    o = 512 * half + 128 * q
                    t = PE(te.transpose, [t_f] + (free if q == 0 else []), P[bank][:, 128 * q:128 * q + 128],
                           Y[i][:, o:o + 128], ident, sig=q == 3)
                yield
                ta = AC(s.activation, [t, t_sq], YT[i][:, 512 * half:512 * half + 512], P[bank][:, :],
                        ACT.Copy)
                give(bank, [ta])
            y_freed[p] = [t]
            t_yt[p] = ta
            if hu == 0:
                return
            for _ in range(3):
                yield
            for half in range(2):
                while not bank_ready():
                    yield
                bank, free = gfree.pop(0)[:2]
                for q in range(4):
                    o = 512 * half + 128 * q
                    for pp in range(2):
                        t = PE(te.matmul, [t_yt[p - 1], ta] + (free if q + pp == 0 else []),
                               P[bank][:, 128 * q:128 * q + 128], YT[pp][:, o:o + 128],
                               Wp[:, 128 * (h - 1 + pp):128 * (h - 1 + pp) + 128], start=pp == 0, stop=pp == 1,
                               sig=q == 3 and pp == 1)
                yield
                yield
                o = 1024 * b + 512 * half
                t_acc = DV(v.tensor_tensor, [t, t_acc], acc[:, o:o + 512], P[bank][:, :], acc[:, o:o + 512], ALU.add)
                give(bank, [t_acc])
            yt_freed[u] = [t]
            if h == KVH - 1:
                finished(b)

        ye_v = ye_d.rearrange("(e a p) c -> e p a c", e=NE, p=128)
        xe_v = xe_d.rearrange("(e a p) c -> e p a c", e=NE, p=128)

        def experts():
            while t_sc[0] is None:
                yield
            up_free = down_free = xe_free = xet_free = ye_free = [t_sc[0], t_wpe[0]] + ffn_done
            for e in range(NE):
                SPD(s_ew, up_free, EW[0], w1[e])
                SPD(s_ew, up_free, EW[1], w3[e])
                t_ew = SPD(s_ew, down_free, EW[2].rearrange("p (c n) -> p c n", c=4),
                           w2[e].rearrange("(c p) n -> p c n", p=128))
                t_xe = SPD(s_xe, xe_free, XE.rearrange("p (a c) -> p a c", c=128), xe_v[e])
                for _ in range(6):
                    yield
                while not bank_ready():
                    yield
                bank, free = gfree.pop(0)[:2]
                for q in range(3):
                    t = PE(te.transpose, [t_xe] + (free if q == 0 else []), P[bank][:, 128 * q:128 * q + 128],
                           XE[:, 128 * q:128 * q + 128], ident, sig=q == 2)
                xe_free = [t]
                yield
                t_x = AC(s.activation, [t] + xet_free, XET, P[bank][:, 0:384], ACT.Identity, scale=GB[:, 0:1],
                         bias=GB[:, 1:2])
                give(bank, [t_x])
                yield
                t_s = []
                for n in range(8):
                    w, f = n // 4, n % 4
                    while not bank_ready():
                        yield
                    bank, free = gfree.pop(0)[:2]
                    t = PE(te.matmul, [t_x, t_ew] + free, P[bank][:, 0:384], EW[w][:, 128 * f:128 * f + 128], XET,
                           start=True, stop=True, sig=True)
                    yield
                    gt = GTe[:, 384 * f:384 * f + 384]
                    if w == 0:
                        t_s.append(AC(s.activation, [t] + down_free, gt, P[bank][:, 0:384], ACT.Silu))
                        give(bank, [t_s[f]])
                    else:
                        t_s[f] = DV(v.tensor_tensor, [t, t_s[f]], gt, gt, P[bank][:, 0:384], ALU.mult)
                        give(bank, [t_s[f]])
                up_free = xet_free = [t]
                yield
                while not bank_ready():
                    yield
                bank, free = gfree.pop(0)[:2]
                for q in range(3):
                    for f in range(4):
                        t = PE(te.matmul, [t_s[f]] + (free if q + f == 0 else []), P[bank][:, 128 * q:128 * q + 128],
                               GTe[:, 384 * f + 128 * q:384 * f + 128 * q + 128], EW[2][:, 128 * f:128 * f + 128],
                               start=f == 0, stop=f == 3, sig=q == 2 and f == 3)
                    if q < 2:
                        yield
                down_free = [t]
                yield
                t = AC(s.activation, [t] + ye_free, YE, P[bank][:, 0:384], ACT.Copy)
                give(bank, [t])
                t_ye = SPD(s_ye, [t], ye_v[e], YE.rearrange("p (a c) -> p a c", c=128))
                ye_free = [t_ye]
                yield
            for _ in range(4):
                yield
            active.append(combine(t_ye))

        def combine(t_ye):
            nonlocal t_acc
            yg_free, t_g = [[] for _ in range(NYG)], {}
            order = [(k, c) for k in range(NBLK) for c in (k, k + 32)]
            for n in range(64 + 2):
                if n < 64:
                    k, c = order[n]
                    i = n % NYG
                    t_g[n] = POD(s_yg[i], g.indirect_dma_start, [t_ye, t_ig[0]] + yg_free[i],
                                 YG[:, 128 * i:128 * i + 128], None, ye_d[:, :],
                                 bass.IndirectOffsetOnAxis(ap=idx_g[:, c:c + 1], axis=0))
                if n >= 2:
                    k, c = order[n - 2]
                    i = (n - 2) % NYG
                    a_ = acc[:, 128 * k:128 * k + 128]
                    t_acc = DV(v.scalar_tensor_tensor, [t_g[n - 2], t_gk[0], t_acc], a_, YG[:, 128 * i:128 * i + 128],
                               gk[:, c:c + 1], a_, ALU.mult, ALU.add)
                    yg_free[i] = [t_acc]
                    if c >= 32 and k % NB == NB - 1:
                        finished(k // NB)
                yield
                yield
                yield
                yield

        def norms():
            for b in range(B):
                yield from norm(b)

        def last_uses():
            toks = [t_acc, t_route[3], t_gate[3]] + gt_free[0] + gt_free[1] + sil_free[0] + sil_free[1]
            for i in range(5):
                toks += bank_free[i]
            return toks

        def first_projection():
            early_done.extend([t_wq[0], t_wpe[0], t_ln[2], t_ln[3], t_xt_pe[2], t_xt_pe[3]])
            for i in range(2):
                t_one.append(DV(v.memset, early_done, Vt[i].rearrange("p (n d) -> p n d", d=64)[:, :, 63:64], 1.0))
            for n in (6, 7):
                give(n, bank_free[n])
            active.extend([first_lane(0), first_lane(1), prep_k(0, 0), prep_k(0, 1), prep_q(0, 0), prep_q(0, 1),
                           first_hrow()])

        def first_lane(i):
            for blk in range(i, NB, 2):
                yield from project(0, blk)

        def first_hrow():
            while t_hd[0] is None:
                yield
            load_hrow(0)

        def begin_attention():
            drain(lambda: t_gk[0] is not None and 0 in t_hr)
            ffn_done.extend(last_uses())
            for n in range(NS, 6):
                give(n, ffn_done if n < 5 else bank_free[5])
            active.append(prep_d(0, 0))
        active.append(norms())
        drain(lambda: 0 in t_ht)
        held, stage = None, 0
        for gi in range(8):
            drain(lambda: gi in t_ht)
            for f in range(4):
                if stage == 0 and 3 in t_gate and 3 in t_route:
                    active += [forget(), route(), weights()]
                    stage = 1
                if stage == 1 and t_wpe[0] is not None:
                    first_projection()
                    stage = 2
                up = chunk(gi, f)
                if held is not None:
                    gate(*held)
                held = up
                if gi > 0 and f in (1, 2):
                    t_down = shared_down(gi - 1, f - 1)
                elif gi > 0 and f == 3:
                    t_acc = shared_add(gi - 1, t_down)
                for _ in range(6):
                    tick()
        gate(*held)
        shared_down(7, 0)
        t_acc = shared_add(7, shared_down(7, 1))
        begin_attention()
        steps = [(p, m, j) for p in range(32) for m in range(4) for j in range(2 * m + 2)]
        t_a, t_run = {}, {}
        a_of = {st: n % NA for n, st in enumerate(steps)}
        run_got = set()
        t_max = {}

        def before(p, m):
            n = 4 * p + m - 3
            return None if n < 0 else (n // 4, n % 4)

        def scores(st, n):
            p, m, j = st
            b, h, u, hu = pair_parts(p)
            qi, ki, si = (4 * p + m) % 3, p % 2, n % NS
            last = j == 2 * m + 1
            cols = 256 if last else 512
            rq = Qt[qi][:, :]
            if last:
                rq = rq.rearrange("p (a t) -> p a t", a=2)[:, :, 128:256]
            w = t_q[p, m] + [t_k[p, 0], t_k[p, 1]] + s_free[si]
            PE(te.matmul, w, P[si][:, 0:cols], Kh[ki][:, 128 * j:128 * j + 128], rq, start=True, stop=False)
            t = PE(te.matmul, [], P[si][:, 0:cols], Kl[ki][:, 128 * j:128 * j + 128], rq, start=False, stop=True,
                   sig=True)
            if last:
                q_free[qi] = [t]
                if m == 3:
                    k_free[ki] = [t]
            ai = a_of[st]
            a_ = A[ai]
            if j < 2 * m:
                c = es_at[m] + 16 * m * b + KVH * j + h
                t1 = AC(s.activation, [t, t_es[0]] + a_free[ai], a_, P[si][:, :], ACT.Square, scale=ES[:, c:c + 1],
                        bias=EB[:, c:c + 1])
            else:
                t1 = AC(s.activation, [t] + a_free[ai], a_[:, 0:cols], P[si][:, 0:cols], ACT.Square, scale=0.125)
            s_free[si] = [t1]
            t_a[st] = t1

        def maxima(st):
            p, m, j = st
            last, ri = j == 2 * m + 1, (4 * p + m) % 3
            a_, t1 = A[a_of[st]], t_a[st]
            qi, cols = (4 * p + m) % 3, 256 if last else 512
            if j >= 2 * m:
                a3 = a_[:, 0:cols].rearrange("p (a t) -> p a t", a=2)
                lo, hi = (256, 384) if last else (0, 256)
                dd = D[qi][:, lo:hi]
                t1 = DV(v.scalar_tensor_tensor, [t1, t_d[p, m]], a3, a3, GUARD * GUARD, bc(dd, 1, 2), ALU.add, ALU.mult)
                if last:
                    d_free[qi] = [t1]
            t_a[st] = t1
            run = RUN[ri]
            r3 = run.rearrange("p (a t) -> p a t", a=2)
            t2 = None
            if j == 1:
                drain(lambda: before(p, m) is None or before(p, m) in run_got)
                a0 = A[a_of[p, m, 0]]
                if m == 0:
                    a03 = a0.rearrange("p (a t) -> p a t", a=2)
                    DV(v.tensor_copy, [t1] + run_free[ri], r3[:, :, 0:128], a03[:, :, 0:128])
                    t2 = DV(v.tensor_tensor, [], r3[:, :, 128:256], a03[:, :, 128:256],
                            a_[:, 0:256].rearrange("p (a t) -> p a t", a=2), ALU.max)
                else:
                    t2 = DV(v.tensor_tensor, [t1, t_a[p, m, 0]] + run_free[ri], run, a0, a_, ALU.max)
            elif last:
                t2 = DV(v.tensor_tensor, [t1, t_run[p, m]], r3[:, :, 128:256], r3[:, :, 128:256],
                        a_[:, 0:256].rearrange("p (a t) -> p a t", a=2), ALU.max)
            elif j > 1:
                t2 = DV(v.tensor_tensor, [t1, t_run[p, m]], run, run, a_, ALU.max)
            if t2 is not None:
                t_run[p, m] = t2
                t_max[st] = t2
                if j == 1:
                    t_max[p, m, 0] = t2
            if last:
                active.append(collect_max(p, m, t2))

        def values(st):
            p, m, j = st
            b, h, u, hu = pair_parts(p)
            last = j == 2 * m + 1
            ai = a_of[st]
            vt = Vt[u % 2].rearrange("p (k n d) -> p k n d", k=NB, d=64)[:, j, hu]
            if j == 0:
                drain(bank_ready)
                o_bank[p, m], free = gfree.pop(0)[:2]
            ob = P[o_bank[p, m]]
            for hd in range(2):
                if last:
                    o, r = ob[64 * hd:64 * hd + 64, 128:256], A[ai][:, 128 * hd:128 * hd + 128]
                else:
                    o, r = ob[64 * hd:64 * hd + 64, 0:256], A[ai][:, 256 * hd:256 * hd + 256]
                t = PE(te.matmul, [t_a[st], t_v[u, j]] + (free if j == 0 else []), o, vt, r, start=j == 0,
                       stop=last, sig=hd == 1)
            a_free[ai] = [t, t_max[st]]
            if last:
                if m == 3 and hu == 1:
                    vt_freed[u] = [t]
                active.append(collect(p, m, t))
                if m == 3:
                    active.append(finish(p))

        side = []
        for n, st in enumerate(steps):
            p, m, j = st
            u, hu = p // 2, p % 2
            if (m, j) == (0, 0):
                if p == 2:
                    active.append(experts())
                drain(lambda: not side and (p, 0) in t_q and (p, 0) in t_k and (p, 1) in t_k)
                if p + 1 < 32:
                    if u + 1 < 16:
                        side += [project(u + 1, blk) for blk in ((0, 1, 2, 3, 4, 5), (6, 7))[hu]]
                    if hu == 0:
                        side.insert(0, load_k(p + 1))
                    else:
                        side += [prep_k(p + 1, 0), prep_k(p + 1, 1)]
            if j == 0:
                for i in ((1, 2) if n == 0 else (2,)):
                    ahead = 4 * p + m + i
                    if ahead < 128:
                        active.append(prep_d(ahead // 4, ahead % 4))
                        if i == 2:
                            active.append(prep_q(ahead // 4, ahead % 4))
            if side and n % 2 == 0:
                active.append(side.pop(0))
            tick()
            drain(lambda: (p, m) in t_q and (p, m) in t_d)
            scores(st, n)
            if n >= 1:
                maxima(steps[n - 1])
            if n >= LAG:
                values(steps[n - LAG])
        for n in range(len(steps), len(steps) + LAG):
            tick()
            if n - 1 < len(steps):
                maxima(steps[n - 1])
            values(steps[n - LAG])
        drain(lambda: not active)

        block = ctx.enter_context(nc.Block())

        def play(eng, name):
            seen = {}
            for f, waits, a, k, sm, by in queues[name]:
                for ws, wv in waits:
                    if seen.get(ws.name, 0) < wv:
                        eng.wait_ge(ws, wv)
                        seen[ws.name] = wv
                ins = f(*a, **k)
                if sm is not None:
                    ins.then_inc(sm, by)

        @block.sync
        def _(eng):
            play(eng, "sp")
            for sm, n in ((s_z, 48), (s_hd, 32), (s_ye, 16 * NE), (s_out, 16 * 8), (s_sc, 16 * 64),
                          (s_kd[0], 16 * 32), (s_kd[1], 16 * 32)):
                eng.wait_ge(sm, n)

        @block.tensor
        def _(eng):
            play(eng, "pe")

        @block.scalar
        def _(eng):
            play(eng, "act")

        @block.vector
        def _(eng):
            play(eng, "dve")

        @block.gpsimd
        def _(eng):
            play(eng, "pool")


def constants():
    k = np.zeros((128, NCONST), np.float32)
    i = np.arange(128)
    k[:, C_ID:C_ID + 128] = np.eye(128)
    k[:, C_UT:C_UT + 128] = i[:, None] <= i[None, :]
    k[:, C_US:C_US + 128] = i[:, None] < i[None, :]
    k[:, C_ONE:C_ONE + 128] = 1.0
    hm = np.zeros((64, 64))
    for j in range(63):
        n = j + 1
        hm[:n, j] = 1.0 / math.sqrt(n * (n + 1))
        hm[n, j] = -n / math.sqrt(n * (n + 1))
    k[0:64, C_H:C_H + 64] = hm
    k[64:128, C_H:C_H + 64] = hm
    k[:, C_IM8:C_IM8 + 8] = np.arange(8) - 8
    k[:, C_I384:C_I384 + 8] = np.arange(8) * SLOT
    div = 2.0 * np.pi / float(T) ** (np.arange(0, HD, 2, dtype=np.float32) / HD)
    ang = (np.arange(T, dtype=np.float32)[:, None] * div.astype(np.float32)[None, :]).astype(np.float64)
    cos, sin = (f(ang).astype(np.float32).reshape(NB, 128, 32).transpose(1, 0, 2) for f in (np.cos, np.sin))
    k[:, C_COS:C_COS + 512] = np.concatenate([cos, cos], axis=2).reshape(128, 512)
    k[:, C_SIN:C_SIN + 512] = np.concatenate([-sin, sin], axis=2).reshape(128, 512)
    return k


def kernel(**inputs):
    import concourse.bacc as bacc
    from concourse.bass_utils import run_bass_kernel_spmd

    w = np.asarray(inputs["L0_attn_w_attn"])
    perm = np.concatenate([np.arange(0, HD, 2), np.arange(1, HD, 2)])
    wq = w[:, 0:1024].reshape(C, 16, HD)[:, :, perm].reshape(C, 4, 256)
    wk = w[:, 1024:1536].reshape(C, 8, HD)[:, :, perm].reshape(C, 4, 128)
    arrays = {
        "x": inputs["L0_attn_x"],
        "w_qkv": np.concatenate([wq, wk], axis=2),
        "w_gate": w[:, 2048:2056],
        "wvT": w[:, 1536:2048].reshape(C, 4, 128).transpose(2, 1, 0),
        "w_proj": inputs["L0_attn_w_proj"],
        "ln_w2": np.asarray(inputs["L0_attn_ln_w"]).reshape(HD, 1),
        "ln_g": np.asarray(inputs["L0_ffn_ln_g"]).reshape(C, 1),
        "ln_b": np.asarray(inputs["L0_ffn_ln_b"]).reshape(C, 1),
        "wr": inputs["L0_ffn_Wr"],
        "w1": inputs["L0_ffn_W1"],
        "w3": inputs["L0_ffn_W3"],
        "w2": inputs["L0_ffn_W2"],
        "w1s": inputs["L0_ffn_W1s"],
        "w3s": inputs["L0_ffn_W3s"],
        "w2s": inputs["L0_ffn_W2s"],
        "const": constants(),
    }
    arrays = {f"in_{n}": np.ascontiguousarray(a) for n, a in arrays.items()}
    nc = bacc.Bacc("TRN2", target_bir_lowering=False, num_devices=1)
    args = [nc.dram_tensor(n, a.shape, mybir.dt.from_np(a.dtype), kind="ExternalInput").ap() for n, a in arrays.items()]
    out = nc.dram_tensor("out_0", (B, T, C), mybir.dt.float32, kind="ExternalOutput").ap()
    block_program(nc, *args, out)
    r = run_bass_kernel_spmd(nc, [arrays], core_ids=[0])
    return r.results[0]["out_0"]
```
